# Optimizing a Trainium2 kernel written in Bass

```python
import numpy as np
import jax
import jax.numpy as jnp

def _softmax(x, axis=-1):
    return jax.nn.softmax(x, axis=axis)

def _gelu(x):
    return jax.nn.gelu(x, approximate=True)

def _silu(x):
    return jax.nn.silu(x)

def _sigmoid(x):
    return jax.nn.sigmoid(x)

def _layernorm(x, axis=-1, eps=1e-05):
    m = jnp.mean(x, axis=axis, keepdims=True)
    v = jnp.var(x, axis=axis, keepdims=True)
    return (x - m) / jnp.sqrt(v + eps)

def _scatter_add(tgt, idx, src, axis=0):
    return tgt.at[idx].add(src)

def _segment_sum(src, seg, n):
    return jax.ops.segment_sum(src, seg, n)
kernel_name = 'mk_gnn_preln_d4_gnn_r64_aed149'

def setup_inputs(seed: int=0):
    np.random.seed(seed)
    _w = jnp.asarray

    def _rec_inputs():
        import jax
        import jax.numpy as jnp
        _gk = jax.random.key(seed)
        x = -0.000202 + 1 * jax.random.normal(jax.random.fold_in(_gk, 1), (100000, 128), jnp.float32)
        src = jax.random.randint(jax.random.fold_in(_gk, 2), (25000,), 0, 100000, jnp.int32)
        dst = jax.random.randint(jax.random.fold_in(_gk, 3), (25000,), 0, 100000, jnp.int32)
        _o = jnp.argsort(dst, stable=True)
        src = src[_o]
        dst = dst[_o]
        edge_attr_16 = 0.000254156 + 0.999948 * jax.random.normal(jax.random.fold_in(_gk, 12), (25000, 16), jnp.float32)
        edge_attr_64 = -9.77346e-05 + 0.999888 * jax.random.normal(jax.random.fold_in(_gk, 13), (25000, 64), jnp.float32)
        return (x, src, dst, edge_attr_16, edge_attr_64)
    x, src, dst, edge_attr_16, edge_attr_64 = _rec_inputs()

    def _L0_gnn_setup():
        import jax, jax.numpy as jnp
        import numpy as np
        N_NODES = 50000
        N_EDGES = 12500
        IN_DIM = 128
        E_FEATS = 64
        H = 8
        D = IN_DIM // H
        NEG_SLOPE = 0.2
        key = jax.random.key(seed)
        ks = jax.random.split(key, 9)
        h = jax.random.normal(ks[0], (N_NODES, IN_DIM), dtype=jnp.float32)
        edge_features = jax.random.normal(ks[1], (N_EDGES, E_FEATS), dtype=jnp.float32)
        src = jax.random.randint(ks[2], (N_EDGES,), 0, N_NODES, dtype=jnp.int32)
        dst = jax.random.randint(ks[3], (N_EDGES,), 0, N_NODES, dtype=jnp.int32)
        s = 0.05
        Wq = jax.random.normal(ks[4], (IN_DIM, IN_DIM), dtype=jnp.float32) * s
        Wk = jax.random.normal(ks[5], (IN_DIM, IN_DIM), dtype=jnp.float32) * s
        Wv = jax.random.normal(ks[6], (IN_DIM, IN_DIM), dtype=jnp.float32) * s
        We = jax.random.normal(ks[7], (H, E_FEATS), dtype=jnp.float32) * s
        Wres = jax.random.normal(ks[8], (IN_DIM, IN_DIM), dtype=jnp.float32) * s
        return {'h': h, 'edge_features': edge_features, 'src': src, 'dst': dst, 'Wq': Wq, 'Wk': Wk, 'Wv': Wv, 'We': We, 'Wres': Wres}
    _L0_gnn_all = _L0_gnn_setup()
    _L0_gnn_in = {k: v for k, v in _L0_gnn_all.items() if k in ('Wq', 'Wk', 'Wv', 'We', 'Wres')}
    del _L0_gnn_all

    def _L1_gnn_setup():
        import jax, jax.numpy as jnp
        import numpy as np
        N_NODES = 100000
        N_EDGES = 12500
        D_IN = 128
        D_OUT = 128
        E_DIM = 16
        key = jax.random.key(seed)
        k1, k2, k3, k4, k5 = jax.random.split(key, 5)
        x = jax.random.normal(k1, (N_NODES, D_IN), dtype=jnp.float32)
        edge_index = jax.random.randint(k2, (2, N_EDGES), 0, N_NODES, dtype=jnp.int64)
        edge_attr = jax.random.normal(k3, (N_EDGES, E_DIM), dtype=jnp.float32)
        W = jax.random.uniform(k4, (D_IN, D_OUT), dtype=jnp.float32, minval=-1.0, maxval=1.0) * float(np.sqrt(6.0 / (D_IN + D_OUT)))
        edge_w = jax.random.uniform(k5, (E_DIM, D_OUT), dtype=jnp.float32, minval=-1.0, maxval=1.0) * float(np.sqrt(6.0 / (E_DIM + D_OUT)))
        b = jnp.zeros((D_OUT,), dtype=jnp.float32)
        return {'x': x, 'edge_index': edge_index, 'edge_attr': edge_attr, 'W': W, 'edge_w': edge_w, 'b': b}
    _L1_gnn_all = _L1_gnn_setup()
    _L1_gnn_in = {k: v for k, v in _L1_gnn_all.items() if k in ('W', 'edge_w', 'b')}
    del _L1_gnn_all

    def _L2_gnn_setup():
        import jax, jax.numpy as jnp
        import numpy as np
        import math
        N, E = (50000, 12500)
        IN_F, OUT_F, H = (128, 128, 8)
        D = math.ceil(OUT_F / H)
        GATE_F = 64

        def _layer_norm(x, g, b, eps=1e-05):
            mu = jnp.mean(x, axis=-1, keepdims=True)
            var = jnp.var(x, axis=-1, keepdims=True)
            return (x - mu) * jax.lax.rsqrt(var + eps) * g + b
        key = jax.random.key(seed)
        ks = jax.random.split(key, 16)

        def lin(k, fi, fo):
            return jax.random.normal(k, (fi, fo), jnp.float32) / np.sqrt(fi)
        return {'h': jax.random.normal(ks[0], (N, IN_F), jnp.float32), 'src': jax.random.randint(ks[1], (E,), 0, N, jnp.int32), 'dst': jax.random.randint(ks[2], (E,), 0, N, jnp.int32), 'ln1_g': jnp.ones((IN_F,), jnp.float32), 'ln1_b': jnp.zeros((IN_F,), jnp.float32), 'W_attn': lin(ks[3], IN_F, H * D), 'W_pool': lin(ks[4], IN_F, IN_F), 'b_pool': jnp.zeros((IN_F,), jnp.float32), 'W_gself': lin(ks[5], IN_F, GATE_F), 'W_gneigh': lin(ks[6], IN_F, GATE_F), 'b_gate': jnp.zeros((GATE_F,), jnp.float32), 'W_gr': lin(ks[7], GATE_F, H), 'b_gr': jnp.zeros((H,), jnp.float32), 'W_hr': lin(ks[8], H * D, OUT_F), 'b_hr': jnp.zeros((OUT_F,), jnp.float32), 'ln2_g': jnp.ones((OUT_F,), jnp.float32), 'ln2_b': jnp.zeros((OUT_F,), jnp.float32), 'W_si': lin(ks[9], OUT_F, OUT_F), 'b_si': jnp.zeros((OUT_F,), jnp.float32)}
    _L2_gnn_all = _L2_gnn_setup()
    _L2_gnn_in = {k: v for k, v in _L2_gnn_all.items() if k in ('ln1_g', 'ln1_b', 'W_attn', 'W_pool', 'b_pool', 'W_gself', 'W_gneigh', 'b_gate', 'W_gr', 'b_gr', 'W_hr', 'b_hr', 'ln2_g', 'ln2_b', 'W_si', 'b_si')}
    del _L2_gnn_all

    def _L3_gnn_setup():
        import jax, jax.numpy as jnp
        import numpy as np
        N = 100000
        DIM = 128
        E = 50000

        def gcn_conv(x, edge_index, W, b):
            n = x.shape[0]
            loop = jnp.arange(n, dtype=edge_index.dtype)
            row = jnp.concatenate([edge_index[0], loop])
            col = jnp.concatenate([edge_index[1], loop])
            deg = jax.ops.segment_sum(jnp.ones_like(col, dtype=x.dtype), col, num_segments=n)
            dinv = jnp.where(deg > 0, jax.lax.rsqrt(deg), 0.0)
            norm = dinv[row] * dinv[col]
            xw = x @ W
            msgs = xw[row] * norm[:, None]
            out = jax.ops.segment_sum(msgs, col, num_segments=n)
            return out + b
        key = jax.random.key(seed)
        k1, k2, k3, k4 = jax.random.split(key, 4)
        x = jax.random.normal(k1, (N, DIM), dtype=jnp.float32)
        edge_index = jax.random.randint(k2, (2, E), 0, N, dtype=jnp.int64)
        W = jax.random.normal(k3, (DIM, DIM), dtype=jnp.float32) * (1.0 / np.sqrt(DIM))
        b = jnp.zeros((DIM,), dtype=jnp.float32)
        return {'x': x, 'edge_index': edge_index, 'W': W, 'b': b}
    _L3_gnn_all = _L3_gnn_setup()
    _L3_gnn_in = {k: v for k, v in _L3_gnn_all.items() if k in ('W', 'b')}
    del _L3_gnn_all
    return {'x': x, 'src': src, 'dst': dst, 'edge_attr_16': edge_attr_16, 'edge_attr_64': edge_attr_64, 'L0_gnn_Wq': _L0_gnn_in['Wq'], 'L0_gnn_Wk': _L0_gnn_in['Wk'], 'L0_gnn_Wv': _L0_gnn_in['Wv'], 'L0_gnn_We': _L0_gnn_in['We'], 'L0_gnn_Wres': _L0_gnn_in['Wres'], 'L1_gnn_W': _L1_gnn_in['W'], 'L1_gnn_edge_w': _L1_gnn_in['edge_w'], 'L1_gnn_b': _L1_gnn_in['b'], 'L2_gnn_ln1_g': _L2_gnn_in['ln1_g'], 'L2_gnn_ln1_b': _L2_gnn_in['ln1_b'], 'L2_gnn_W_attn': _L2_gnn_in['W_attn'], 'L2_gnn_W_pool': _L2_gnn_in['W_pool'], 'L2_gnn_b_pool': _L2_gnn_in['b_pool'], 'L2_gnn_W_gself': _L2_gnn_in['W_gself'], 'L2_gnn_W_gneigh': _L2_gnn_in['W_gneigh'], 'L2_gnn_b_gate': _L2_gnn_in['b_gate'], 'L2_gnn_W_gr': _L2_gnn_in['W_gr'], 'L2_gnn_b_gr': _L2_gnn_in['b_gr'], 'L2_gnn_W_hr': _L2_gnn_in['W_hr'], 'L2_gnn_b_hr': _L2_gnn_in['b_hr'], 'L2_gnn_ln2_g': _L2_gnn_in['ln2_g'], 'L2_gnn_ln2_b': _L2_gnn_in['ln2_b'], 'L2_gnn_W_si': _L2_gnn_in['W_si'], 'L2_gnn_b_si': _L2_gnn_in['b_si'], 'L3_gnn_W': _L3_gnn_in['W'], 'L3_gnn_b': _L3_gnn_in['b']}

def reference(x, src, dst, edge_attr_16, edge_attr_64, L0_gnn_Wq, L0_gnn_Wk, L0_gnn_Wv, L0_gnn_We, L0_gnn_Wres, L1_gnn_W, L1_gnn_edge_w, L1_gnn_b, L2_gnn_ln1_g, L2_gnn_ln1_b, L2_gnn_W_attn, L2_gnn_W_pool, L2_gnn_b_pool, L2_gnn_W_gself, L2_gnn_W_gneigh, L2_gnn_b_gate, L2_gnn_W_gr, L2_gnn_b_gr, L2_gnn_W_hr, L2_gnn_b_hr, L2_gnn_ln2_g, L2_gnn_ln2_b, L2_gnn_W_si, L2_gnn_b_si, L3_gnn_W, L3_gnn_b):
    import jax
    import jax.numpy as jnp

    def _L0_gnn_ref(h, edge_features, src, dst, Wq, Wk, Wv, We, Wres):
        import jax, jax.numpy as jnp
        import numpy as np
        N_NODES = 50000
        N_EDGES = 12500
        IN_DIM = 128
        E_FEATS = 64
        H = 8
        D = IN_DIM // H
        NEG_SLOPE = 0.2
        N = h.shape[0]
        q = (h @ Wq.T).reshape(N, H, D)
        k = (h @ Wk.T).reshape(N, H, D)
        v = (h @ Wv.T).reshape(N, H, D)
        _ee = edge_features @ We.T
        e = jnp.einsum('ehd,ehd->eh', q[dst], k[src])
        e = jnp.where(e >= 0, e, NEG_SLOPE * e)
        m = jax.ops.segment_max(e, dst, num_segments=N)
        ex = jnp.exp(e - m[dst])
        z = jax.ops.segment_sum(ex, dst, num_segments=N)
        alpha = ex / z[dst]
        msg = v[src] * alpha[:, :, None]
        rst = jax.ops.segment_sum(msg, dst, num_segments=N)
        rst = rst.reshape(N, H * D)
        rst = rst + h @ Wres.T
        return rst

    def _L1_gnn_ref(x, edge_index, edge_attr, W, edge_w, b):
        import jax, jax.numpy as jnp
        import numpy as np
        N_NODES = 100000
        N_EDGES = 12500
        D_IN = 128
        D_OUT = 128
        E_DIM = 16
        src, dst = (edge_index[0], edge_index[1])
        xw = x @ W
        ew = edge_attr @ edge_w
        msg = xw[src] * ew
        out = jax.ops.segment_sum(msg, dst, num_segments=x.shape[0])
        out = out + b
        return out

    def _L2_gnn_ref(h, src, dst, ln1_g, ln1_b, W_attn, W_pool, b_pool, W_gself, W_gneigh, b_gate, W_gr, b_gr, W_hr, b_hr, ln2_g, ln2_b, W_si, b_si):
        import jax, jax.numpy as jnp
        import numpy as np
        import math
        N, E = (50000, 12500)
        IN_F, OUT_F, H = (128, 128, 8)
        D = math.ceil(OUT_F / H)
        GATE_F = 64

        def _layer_norm(x, g, b, eps=1e-05):
            mu = jnp.mean(x, axis=-1, keepdims=True)
            var = jnp.var(x, axis=-1, keepdims=True)
            return (x - mu) * jax.lax.rsqrt(var + eps) * g + b
        n = h.shape[0]
        h = _layer_norm(h, ln1_g, ln1_b)
        h_skip = h
        ft = (h @ W_attn).reshape(n, H, D)
        e = jnp.sum(ft[src] * ft[dst], axis=-1) / np.sqrt(D)
        m = jax.ops.segment_max(e, dst, num_segments=n)
        ex = jnp.exp(e - m[dst])
        z = jax.ops.segment_sum(ex, dst, num_segments=n)
        alpha = ex / z[dst]
        agg = jax.ops.segment_sum(ft[src] * alpha[:, :, None], dst, num_segments=n)
        h_att = jax.nn.elu(agg)
        p = jax.nn.relu(h_skip @ W_pool + b_pool)
        pm = jax.ops.segment_max(p[src], dst, num_segments=n)
        pm = jnp.where(jnp.isneginf(pm), 0.0, pm)
        gate_feat = h_skip @ W_gself + pm @ W_gneigh + b_gate
        gate = jax.nn.sigmoid(gate_feat @ W_gr + b_gr)
        h_att = h_att * gate[:, :, None]
        h2 = h_att.reshape(n, H * D) @ W_hr + b_hr + h_skip
        h2 = _layer_norm(h2, ln2_g, ln2_b)
        out = jax.nn.elu(h2 @ W_si + b_si) + h2
        return out

    def _L3_gnn_ref(x, edge_index, W, b):
        import jax, jax.numpy as jnp
        import numpy as np
        N = 100000
        DIM = 128
        E = 50000

        def gcn_conv(x, edge_index, W, b):
            n = x.shape[0]
            loop = jnp.arange(n, dtype=edge_index.dtype)
            row = jnp.concatenate([edge_index[0], loop])
            col = jnp.concatenate([edge_index[1], loop])
            deg = jax.ops.segment_sum(jnp.ones_like(col, dtype=x.dtype), col, num_segments=n)
            dinv = jnp.where(deg > 0, jax.lax.rsqrt(deg), 0.0)
            norm = dinv[row] * dinv[col]
            xw = x @ W
            msgs = xw[row] * norm[:, None]
            out = jax.ops.segment_sum(msgs, col, num_segments=n)
            return out + b
        return jax.nn.relu(gcn_conv(x, edge_index, W, b))
    edge_index = jnp.stack([src, dst])
    h = jnp.maximum(_layernorm(x, axis=-1), 0.0)
    x = x + _L0_gnn_ref(h, edge_attr_64, src, dst, L0_gnn_Wq, L0_gnn_Wk, L0_gnn_Wv, L0_gnn_We, L0_gnn_Wres)
    h = jnp.maximum(_layernorm(x, axis=-1), 0.0)
    x = x + _L1_gnn_ref(h, edge_index, edge_attr_16, L1_gnn_W, L1_gnn_edge_w, L1_gnn_b)
    h = jnp.maximum(_layernorm(x, axis=-1), 0.0)
    x = x + _L2_gnn_ref(h, src, dst, L2_gnn_ln1_g, L2_gnn_ln1_b, L2_gnn_W_attn, L2_gnn_W_pool, L2_gnn_b_pool, L2_gnn_W_gself, L2_gnn_W_gneigh, L2_gnn_b_gate, L2_gnn_W_gr, L2_gnn_b_gr, L2_gnn_W_hr, L2_gnn_b_hr, L2_gnn_ln2_g, L2_gnn_ln2_b, L2_gnn_W_si, L2_gnn_b_si)
    h = jnp.maximum(_layernorm(x, axis=-1), 0.0)
    x = x + _L3_gnn_ref(h, edge_index, L3_gnn_W, L3_gnn_b)
    return x

_drawn_inputs = setup_inputs


def setup_inputs(seed=0):
    import zlib

    import numpy as np

    out = dict(_drawn_inputs(seed))
    spreads = {'L1_gnn_b': (0.0, 0.1),
     'L2_gnn_ln1_g': (1.0, 0.2),
     'L2_gnn_ln1_b': (0.0, 0.1),
     'L2_gnn_b_pool': (0.0, 2.0),
     'L2_gnn_b_gate': (0.0, 0.8),
     'L2_gnn_b_gr': (0.0, 2.0),
     'L2_gnn_b_hr': (0.0, 0.1),
     'L2_gnn_ln2_g': (1.0, 0.2),
     'L2_gnn_ln2_b': (0.0, 0.1),
     'L2_gnn_b_si': (0.0, 0.1),
     'L3_gnn_b': (0.0, 0.271)}
    factors = {'L0_gnn_Wq': 7.073, 'L0_gnn_Wk': 7.309}
    for name, (base, spread) in spreads.items():
        noise = np.random.default_rng([zlib.crc32(name.encode()), seed]).standard_normal(out[name].shape)
        drawn = base * np.exp(spread * noise) if base else spread * noise
        out[name] = jnp.asarray(drawn.astype(out[name].dtype))
    for name, factor in factors.items():
        out[name] = (out[name] * factor).astype(out[name].dtype)
    return out
```

```python
from contextlib import ExitStack

import concourse.bass as bass
from concourse import mybir

P = 128
C = 128
W = 8
H = 4
EW = 4
EG = EW * P
U = 4
DH = 16
SLOPE = 0.2
EPS = 1e-5
NEG = -1.0e30
BIG = float(1 << 22)

ALU = mybir.AluOpType
ACT = mybir.ActivationFunctionType
AX = mybir.AxisListType
F32 = mybir.dt.float32
BF16 = mybir.dt.bfloat16
I32 = mybir.dt.int32


class Chain:

    def __init__(self, eng, sem, steps):
        self.eng, self.sem, self.steps = eng, sem, steps

    def start(self, g):
        self.g, self.n = g, 0

    def goes_on(self, g):
        self.g = g

    def mark(self, ins):
        ins.then_inc(self.sem, 1)
        self.n += 1
        return self.n

    def wait(self, n=None):
        self.eng.wait_ge(self.sem, self.g * self.steps + (n or self.n))

    def link(self, ins):
        self.mark(ins)
        self.wait()

    def end(self):
        assert self.n == self.steps, (self.n, self.steps)


class Phase:

    def __init__(self, nc):
        self.nc, self.semaphores = nc, []

    def semaphore(self, name):
        self.semaphores.append(self.nc.alloc_semaphore(name=name))
        return self.semaphores[-1]

    def __enter__(self):
        return self

    def __exit__(self, *error):
        if error[0] is None:
            self.nc.clear_and_free_semaphores(self.semaphores)
            self.nc.all_engine_barrier()


def wait(eng, sem, value):
    if not isinstance(value, int) or value > 0:
        eng.wait_ge(sem, value)


def pipeline(eng, lanes, steps, total, work):
    behind = [h * steps // lanes for h in range(lanes)]
    count = -(-total // lanes)

    def exists(i, h):
        return not isinstance(i, int) or 0 <= i and i * lanes + h < total

    def turn(i):
        for slot in range(steps):
            for h in range(lanes):
                step, at = slot - behind[h], i
                if step < 0:
                    step, at = step + steps, i - 1
                if step in work and exists(at, h):
                    work[step](at, h)

    turn(0)
    turn(1)
    with eng.Fori(2, count - 1) as i:
        turn(i)
    turn(count - 1)
    turn(count)


def flat(t):
    return t.rearrange("p w c -> p (w c)")


def bass_gnn(nc, a, out):
    N = a["x"].shape[0]
    E = a["src"].shape[0]
    GN = P * W
    nodes = -(-N // GN)
    groups = -(-E // (EG * U)) * U
    EP = groups * EG
    T = EP // P
    L = EP // P

    def dram(name, shape, dt=F32):
        return nc.dram_tensor(name, shape, dt).ap()

    t_x1 = dram("t_x1", [N, C])
    t_n2 = dram("t_n2", [N, C])
    t_n3 = dram("t_n3", [N, C])
    x1_e = dram("x1_e", [EP, C])
    x2_e = dram("x2_e", [EP, C])
    x3_e = dram("x3_e", [EP, C])
    n3_e = dram("n3_e", [EP, C])
    attr_e = dram("attr_e", [EP, 16])
    masks = dram("masks", [2, EP])
    lin = dram("lin", [4, EP])

    with ExitStack() as top:
        def sb(name, shape, dt=F32, ctx=top):
            return ctx.enter_context(nc.sbuf_tensor(name, shape, dt))

        ident = sb("ident", [P, P])
        heads = sb("heads", [P, P])
        wqkv = sb("wqkv", [P, 3, C])
        wres0 = sb("wres0", [P, C])
        w1 = sb("w1", [P, C])
        edge_w = sb("edge_w", [16, C])
        wattn = sb("wattn", [P, C])
        wpool = sb("wpool", [P, C])
        wgself = sb("wgself", [P, 64])
        wgneigh = sb("wgneigh", [P, 64])
        wgr = sb("wgr", [64, C])
        whr = sb("whr", [P, C])
        wsi = sb("wsi", [P, C])
        w3 = sb("w3", [P, C])
        ones3 = sb("ones3", [3, P], BF16)
        bias3 = sb("bias3", [3, C], BF16)
        biassi = sb("biassi", [3, C], BF16)
        biashr = sb("biashr", [3, C], BF16)
        b3rows = sb("b3rows", [P, C])
        cols = sb("cols", [P, 8])
        B1, G1, S1, G2, S2, BPOOL, NBGR = range(7)
        b1rows = sb("b1rows", [P, C])
        g1rows = sb("g1rows", [P, C])
        hrrows = sb("hrrows", [P, C])
        bgate = sb("bgate", [64, 1])
        half = sb("half", [P, W])
        src_i = sb("src_i", [P, T], I32)
        dst_i = sb("dst_i", [P, T], I32)
        scat_i = sb("scat_i", [P, T], I32)
        dinv = sb("dinv", [P, T])
        ps = [top.enter_context(nc.psum_tensor(f"ps{h}", [P, 4 * 512], F32)) for h in range(2)]

        def bank(h, k, n=1):
            return ps[h][:, 512 * k:512 * (k + n)]

        def col(k, p=P):
            return cols[0:p, k:k + 1]

        with Phase(nc) as phase, ExitStack() as ctx:
            def sem(name):
                return phase.semaphore(name)

            raw = sb("raw", [P, 4, C], F32, ctx)
            rows = sb("bias_rows", [1, 3, C], F32, ctx)
            part = sb("bias_part", [1, 3, 3, C], BF16, ctx)
            left = sb("bias_left", [1, 3, C], F32, ctx)
            wgr8 = sb("wgr8", [64, 8], F32, ctx)
            bgr8 = sb("bgr8", [8, 1], F32, ctx)
            head8 = sb("head8", [8, P], F32, ctx)
            hrrows2 = sb("hrrows2", [P, C], F32, ctx)
            ints = sb("ints", [P, 4, L], I32, ctx)
            val = sb("val", [P, 4, L], F32, ctx)
            same = sb("same", [P, L], F32, ctx)
            more = sb("more", [P, L], F32, ctx)
            one = sb("one", [P, L], F32, ctx)
            halfl = sb("halfl", [P, L], F32, ctx)
            count = sb("count", [P, L], F32, ctx)
            mask2 = sb("mask2", [P, 2, L], F32, ctx)
            tabs = sb("tabs", [P, 4, L], F32, ctx)
            ends = sb("ends", [P, 2], F32, ctx)
            line = sb("line", [1, 4, P], F32, ctx)
            carry = sb("carry", [P, 1], F32, ctx)
            back = sb("back", [T // 2, 4, 2, P], F32, ctx)
            loaded, edges_in, filled, spread = sem("loaded"), sem("edges_in"), sem("filled"), sem("spread")
            tabled, reloaded, pool_ok, pe_ok = sem("tabled"), sem("reloaded"), sem("pool_ok"), sem("pe_ok")
            parts_ready, ends_ready, line_ready = sem("parts_ready"), sem("ends_ready"), sem("line_ready")
            count_ready, dinv_ready, link = sem("count_ready"), sem("dinv_ready"), sem("link")
            block = ctx.enter_context(nc.Block())
            FULL, REST = E // L, E % L
            blank = sb("blank", [P, (EP - E) * 16 // P], F32, ctx)
            blanked, attr_in = sem("blanked"), sem("attr_in")
            assert (EP - E) * 16 % P == 0

            loads = [(raw[:, k, :], a["L0_gnn_" + n]) for k, n in enumerate(("Wq", "Wk", "Wv", "Wres"))]
            loads += [(w1[:, :], a["L1_gnn_W"]), (edge_w[:, :], a["L1_gnn_edge_w"]),
                      (wattn[:, :], a["L2_gnn_W_attn"]), (wpool[:, :], a["L2_gnn_W_pool"]),
                      (wgself[:, :], a["L2_gnn_W_gself"]), (wgneigh[:, :], a["L2_gnn_W_gneigh"]),
                      (wgr8[:, :], a["L2_gnn_W_gr"]), (whr[:, :], a["L2_gnn_W_hr"]), (wsi[:, :], a["L2_gnn_W_si"]),
                      (w3[:, :], a["L3_gnn_W"])]
            loads += [(rows[:, k, :], a[n].rearrange("(o c) -> o c", o=1))
                      for k, n in enumerate(("L3_gnn_b", "L2_gnn_b_si", "L2_gnn_b_hr"))]
            loads += [(t[:, :], a[n].rearrange("(o c) -> o c", o=1).to_broadcast([P, C])) for t, n in (
                (b3rows, "L3_gnn_b"), (b1rows, "L1_gnn_b"), (g1rows, "L2_gnn_ln1_g"), (hrrows, "L2_gnn_ln1_b"),
                (hrrows2, "L2_gnn_b_hr"))]
            loads += [(d, a[n].rearrange("(c o) -> c o", o=1)) for d, n in (
                (col(B1), "L1_gnn_b"), (col(G1), "L2_gnn_ln1_g"), (col(S1), "L2_gnn_ln1_b"),
                (col(G2), "L2_gnn_ln2_g"), (col(S2), "L2_gnn_ln2_b"), (col(BPOOL), "L2_gnn_b_pool"),
                (bgate[:, :], "L2_gnn_b_gate"), (bgr8[:, :], "L2_gnn_b_gr"))]
            nload = len(loads)

            def edge_loads():
                d, s = a["dst"], a["src"]
                for k, t in ((0, d), (3, s)):
                    yield ints[0:FULL, k, :], t[0:FULL * L].rearrange("(p l) -> p l", l=L)
                    if REST:
                        yield ints[FULL:FULL + 1, k, 0:REST], t[FULL * L:E].rearrange("(o l) -> o l", o=1)
                yield ints[0:1, 1, 1:L], d[0:L - 1].rearrange("(o l) -> o l", o=1)
                yield ints[1:FULL, 1, :], d[L - 1:FULL * L - 1].rearrange("(p l) -> p l", l=L)
                yield ints[FULL:FULL + 1, 1, 0:REST], d[FULL * L - 1:E - 1].rearrange("(o l) -> o l", o=1)
                yield ints[0:FULL, 2, :], d[1:FULL * L + 1].rearrange("(p l) -> p l", l=L)
                yield ints[FULL:FULL + 1, 2, 0:REST - 1], d[FULL * L + 1:E].rearrange("(o l) -> o l", o=1)

            edge_list = list(edge_loads())

            @block.sync
            def _(sp):
                sp.wait_ge(filled, 4)
                sp.dma_start(attr_e[0:E, :], a["edge_attr_16"]).then_inc(attr_in, 16)
                sp.wait_ge(blanked, 1)
                sp.dma_start(attr_e[E:EP, :].rearrange("e c -> (e c)").rearrange("(p k) -> p k", p=P), blank[:, :]
                             ).then_inc(attr_in, 16)
                for dst, src in edge_list:
                    sp.dma_start(dst, src).then_inc(edges_in, 16)
                with nc.allow_non_contiguous_dma(reason="a few columns of weights' length"):
                    for dst, src in loads:
                        sp.dma_start(dst, src).then_inc(loaded, 16)
                sp.wait_ge(parts_ready, 1)
                for k, dst in enumerate((bias3, biassi, biashr)):
                    for j in range(3):
                        sp.dma_start(dst[j:j + 1, :], part[:, k, j, :]).then_inc(spread, 16)
                sp.wait_ge(count_ready, 1)
                sp.wait_ge(dinv_ready, 1)
                for k in range(2):
                    sp.dma_start(masks[k].rearrange("(p l) -> p l", p=P), mask2[:, k, :]).then_inc(tabled, 16)
                for k in range(4):
                    sp.dma_start(lin[k].rearrange("(p l) -> p l", p=P), tabs[:, k, :]).then_inc(tabled, 16)
                sp.wait_ge(tabled, 16 * 6)
                for k in range(4):
                    for j in range(2):
                        sp.dma_start(back[:, k, j, :],
                                     lin[k].rearrange("(j t p) -> j t p", j=2, p=P)[j]).then_inc(reloaded, 16)
                sp.wait_ge(attr_in, 32)
                sp.wait_ge(spread, 16 * 9)
                sp.wait_ge(reloaded, 16 * 8)

            @block.gpsimd
            def _(g):
                g.memset(ident[:, :], 0.0).then_inc(pool_ok, 1)
                g.memset(heads[:, :], 1.0).then_inc(pool_ok, 1)
                g.memset(head8[:, :], 1.0).then_inc(pool_ok, 1)
                g.memset(half[:, :], -0.5).then_inc(pool_ok, 1)
                g.memset(halfl[:, :], -0.5).then_inc(pool_ok, 1)
                g.wait_ge(pool_ok, 5)
                g.affine_select(out=ident[:, :], in_=ident[:, :], compare_op=ALU.not_equal, fill=1.0, base=0,
                                pattern=[[-1, P]], channel_multiplier=1).then_inc(pool_ok, 1)

                def in_head(t, first, sign, wait_for):
                    g.wait_ge(pool_ok, wait_for)
                    v = t[:, :].rearrange("p (h d) -> p h d", d=DH)
                    step, inner, mult = first
                    base = 0 if sign > 0 else DH - 1
                    g.affine_select(out=v, in_=v, compare_op=ALU.is_ge, fill=0.0, base=base,
                                    pattern=[[sign * step, P // DH], [sign * inner, DH]],
                                    channel_multiplier=sign * mult).then_inc(pool_ok, 1)
                in_head(heads, (-DH, 0, 1), 1, 6)
                in_head(heads, (-DH, 0, 1), -1, 7)
                in_head(head8, (DH, 1, -DH), 1, 8)
                in_head(head8, (DH, 1, -DH), -1, 9)
                g.wait_ge(count_ready, 1)
                g.tensor_tensor(tabs[:, 3, :], count[:, :], halfl[:, :], ALU.pow).then_inc(dinv_ready, 1)

            @block.tensor
            def _(pe):
                pe.wait_ge(pool_ok, 10)
                pe.wait_ge(loaded, 16 * nload)
                for k in range(4):
                    ins = pe.transpose(ps[0][:, k * C:(k + 1) * C], raw[:, k, :], ident[:, :])
                ins.then_inc(pe_ok, 1)
                pe.matmul(ps[1][:, 0:1], head8[:, :], bgr8[:, :], start=True, stop=True).then_inc(pe_ok, 1)
                pe.wait_ge(ends_ready, 1)
                pe.transpose(ps[1][0:1, 512:512 + P], ends[:, 0:1], ident[:, :])
                pe.transpose(ps[1][0:1, 512 + P:512 + 2 * P], ends[:, 1:2], ident[:, :]).then_inc(pe_ok, 1)
                pe.wait_ge(line_ready, 1)
                pe.transpose(ps[1][:, 1024:1025], line[0:1, 3, :], ident[0:1, 0:1]).then_inc(pe_ok, 1)
                pe.wait_ge(reloaded, 16 * 8)
                for k in range(4):
                    for j in range(2):
                        o = 256 * k + (T // 2) * j
                        ins = pe.transpose(ps[0][:, 1024 + o:1024 + o + T // 2], back[:, k, j, :],
                                           ident[0:T // 2, 0:T // 2])
                ins.then_inc(pe_ok, 1)

            @block.vector
            def _(v):
                ch = Chain(v, link, 35)
                ch.start(0)
                v.memset(blank[:, :], 0.0).then_inc(blanked, 1)
                for k, value in ((0, N), (1, -1), (2, -1), (3, 0)):
                    v.memset(ints[:, k, :], value).then_inc(filled, 1)
                ch.mark(v.memset(one[:, :], 1.0))
                ch.mark(v.memset(ones3[:, :], 1.0))
                ch.mark(v.memset(line[:, :, :], 0.0))
                v.wait_ge(edges_in, 16 * len(edge_list))
                v.wait_ge(filled, 4)
                ch.link(v.tensor_copy(val[:, :, :], ints[:, :, :]))
                ch.mark(v.tensor_tensor(same[:, :], val[:, 0, :], val[:, 1, :], ALU.is_equal))
                ch.link(v.tensor_tensor(more[:, :], val[:, 0, :], val[:, 2, :], ALU.is_equal))
                ch.mark(v.tensor_tensor_scan(count[:, :], same[:, :], one[:, :], 0.0, ALU.mult, ALU.add))
                ch.mark(v.tensor_reduce(ends[:, 1:2], same[:, :], AX.X, ALU.min))
                ch.wait()
                ch.link(v.tensor_copy(ends[:, 0:1], count[:, L - 1:L]))
                v.sem_inc(ends_ready, 1)
                v.wait_ge(loaded, 16 * nload)
                ch.mark(v.tensor_copy(left[:, 0, :], rows[:, 0, :]))
                ch.mark(v.tensor_copy(left[:, 2, :], rows[:, 2, :]))
                ch.link(v.tensor_scalar(left[:, 1, :], rows[:, 1, :], 1.0, None, ALU.add))
                for j in range(3):
                    ch.link(v.tensor_copy(part[:, :, j, :], left[:, :, :]))
                    if j < 2:
                        ch.link(v.tensor_tensor(left[:, :, :], left[:, :, :], part[:, :, j, :], ALU.subtract))
                v.sem_inc(parts_ready, 1)
                ch.mark(v.scalar_tensor_tensor(out=tabs[:, 2, :], in0=more[:, :], scalar=BIG, in1=val[:, 0, :],
                                               op0=ALU.mult, op1=ALU.add))
                ch.mark(v.tensor_copy(tabs[:, 0, :], val[:, 3, :]))
                ch.mark(v.tensor_copy(tabs[:, 1, :], val[:, 0, :]))
                ch.mark(v.tensor_copy(mask2[:, 0, :], same[:, :]))
                ch.link(v.tensor_scalar(mask2[:, 1, :], same[:, :], 1.0, -NEG, ALU.subtract, ALU.mult))
                v.wait_ge(pe_ok, 3)
                ch.link(v.tensor_copy(line[:, 0:2, :], ps[1][0:1, 512:512 + 2 * P].rearrange("p (k c) -> p k c", k=2)))
                ch.link(v.tensor_tensor_scan(line[:, 2, :], line[:, 1, :], line[:, 0, :], 0.0, ALU.mult, ALU.add))
                ch.link(v.tensor_copy(line[:, 3, 1:P], line[:, 2, 0:P - 1]))
                v.sem_inc(line_ready, 1)
                v.wait_ge(pe_ok, 4)
                ch.link(v.tensor_copy(carry[:, :], ps[1][:, 1024:1025]))
                ch.link(v.tensor_tensor_scan(count[:, :], same[:, :], one[:, :], carry[:, :], ALU.mult, ALU.add))
                ch.link(v.tensor_scalar(count[:, :], count[:, :], 1.0, None, ALU.add))
                v.sem_inc(count_ready, 1)
                v.tensor_copy(wqkv[:, :, :], ps[0][:, 0:3 * C].rearrange("p (k c) -> p k c", k=3))
                v.tensor_copy(wres0[:, :], ps[0][:, 3 * C:4 * C])
                v.tensor_scalar(col(NBGR), ps[1][:, 0:1], -1.0, None, ALU.mult)
                v.tensor_copy(wgr[:, :].rearrange("p (h d) -> p h d", d=DH),
                              wgr8[:, :].rearrange("p (h o) -> p h o", o=1).to_broadcast([64, 8, DH]))
                v.tensor_tensor(hrrows[:, :], hrrows[:, :], hrrows2[:, :], ALU.add)
                v.wait_ge(pe_ok, 5)
                for k, t in enumerate((src_i, dst_i, scat_i, dinv)):
                    v.tensor_copy(t[:, :].rearrange("p (j t) -> p j t", j=2),
                                  ps[0][:, 1024 + 256 * k:1024 + 256 * k + T].rearrange("p (j t) -> p j t", j=2))

        with Phase(nc) as phase, ExitStack() as ctx:
            def sem(name):
                return phase.semaphore("node_" + name)

            def bufs(name, shape, dt=F32):
                return [sb(f"{name}{h}", shape, dt, ctx) for h in range(H)]

            x0 = bufs("x0", [P, W, C])
            n0 = bufs("n0", [P, W, C])
            hT = bufs("hT", [P, W, C])
            x1 = bufs("x1", [P, W, C])
            x2 = bufs("x2", [P, W, C])
            u = bufs("u", [P, W, C])
            n2 = bufs("n2", [P, W, C])
            x3 = bufs("x3", [P, W, C])
            st = bufs("st", [P, W, 6])
            small = bufs("small", [P, 8, W])
            SUM, DIF, M2, NMEAN, VAR, EPS2, RSTD, NB = range(8)

            NK = 5
            K0, K2A, K2B, KH, K3 = range(NK)
            x_loaded = [sem(f"x_loaded{h}") for h in range(H)]
            var_ready = [sem(f"var_ready{k}") for k in range(NK)]
            rstd_ready = [sem(f"rstd_ready{k}") for k in range(NK)]
            rows_ready = [sem(f"rows_ready{k}") for k in range(NK)]
            t_ready = [sem(f"t_ready{k}") for k in range(NK)]
            hT_ready = [sem(f"hT_ready{k}") for k in range(NK)]
            mm_ready = [sem(f"mm_ready{k}") for k in range(NK)]
            x1_ready, x2_ready, h2_ready = sem("x1_ready"), sem("x2_ready"), sem("h2_ready")
            y_ready, y_used = sem("y_ready"), sem("y_used")
            exp_ready, w_ready = sem("exp_ready"), sem("w_ready")
            x3_ready, out_ready = sem("x3_ready"), sem("out_ready")
            x1_stored = [sem(f"x1_stored{h}") for h in range(H)]
            n2_stored = [sem(f"n2_stored{h}") for h in range(H)]
            out_stored = [sem(f"out_stored{h}") for h in range(H)]
            dve_chain = [sem(f"dve_chain{h}") for h in range(H)]
            pool_chain = [sem(f"pool_chain{h}") for h in range(H)]
            block = ctx.enter_context(nc.Block())

            (LOAD, STATS0, ROOT0, NORM0, TURN0, RELU0, RES0, X1, X2, STATS2, ROOT2, NORM2, H2, STATSH, ROOTH, NORMH,
             TURNH, Y, X3, Z, EXPZ, ELU, X3SUM, STATS3, ROOT3, NORM3, TURN3, RELU3, OUT3, OUT, STEPS) = range(31)

            def bk(h):
                return ps[h // 2][:, 1024 * (h % 2):1024 * (h % 2) + 1024]

            def tile(h, w):
                return bk(h)[:, w * C:(w + 1) * C]

            def last(i, h):
                return isinstance(i, int) and i * H + h == nodes - 1

            def node_rows(t, i, h):
                start = N - GN if last(i, h) else (i * H + h) * GN
                return t.rearrange("n c -> (n c)")[bass.ds(start * C, GN * C)].rearrange("(p w) -> p w", p=P)

            @block.sync
            def _(sp):
                def load(i, h):
                    wait(sp, x1_ready, (i - 1) * H + h + 1)
                    sp.dma_start(flat(x0[h]), node_rows(a["x"], i, h)).then_inc(x_loaded[h], 16)

                def store(i, h, table, src, ready, stored, per_turn, nth):
                    sp.wait_ge(ready, i * H + h + 1)
                    if last(i, h):
                        sp.wait_ge(stored[(h - 1) % H], 16 * (per_turn * (i - (h == 0)) + nth))
                    sp.dma_start(node_rows(table, i, h), flat(src[h])).then_inc(stored[h], 16)

                pipeline(sp, H, STEPS, nodes, {
                    LOAD: load,
                    X1: lambda i, h: store(i, h, t_x1, x1, x1_ready, x1_stored, 1, 1),
                    NORM2: lambda i, h: store(i, h, t_n2, n2, rows_ready[K2B], n2_stored, 2, 1),
                    NORM3: lambda i, h: store(i, h, t_n3, n2, rows_ready[K3], n2_stored, 2, 2),
                    OUT: lambda i, h: store(i, h, out, x3, out_ready, out_stored, 1, 1),
                })
                for h in range(H):
                    done = -(-(nodes - h) // H)
                    sp.wait_ge(x1_stored[h], 16 * done)
                    sp.wait_ge(n2_stored[h], 32 * done)
                    sp.wait_ge(out_stored[h], 16 * done)

            @block.scalar
            def _(act):
                def normalise(i, h, k, dst, src):
                    at = i * H + h + 1
                    act.wait_ge(rstd_ready[k], at)
                    if k == K0:
                        wait(act, t_ready[KH], at - H)
                    if k == K2B:
                        wait(act, n2_stored[h], 32 * i)
                        wait(act, t_ready[K3], at - H)
                    if k == K3:
                        act.wait_ge(n2_stored[h], 32 * i + 16)
                        act.wait_ge(h2_ready, at)
                    for w in range(W):
                        ins = act.activation(dst[h][:, w, :], src[h][:, w, :], ACT.Identity,
                                             scale=small[h][:, RSTD, w:w + 1], bias=small[h][:, NB, w:w + 1])
                    ins.then_inc(rows_ready[k], 1)

                def relu_t(i, h, k):
                    act.wait_ge(t_ready[k], i * H + h + 1)
                    act.activation(flat(hT[h]), bk(h), ACT.Relu).then_inc(hT_ready[k], 1)

                def y_t(i, h):
                    act.wait_ge(t_ready[KH], i * H + h + 1)
                    act.activation(flat(hT[h]), bk(h), ACT.Identity, scale=col(G2), bias=col(S2)
                                   ).then_inc(hT_ready[KH], 1)

                def exp_z(i, h):
                    act.wait_ge(mm_ready[KH], i * H + h + 1)
                    act.activation(flat(u[h]), bk(h), ACT.Exp, bias=-1.0).then_inc(exp_ready, 1)

                pipeline(act, H, STEPS, nodes, {
                    NORM0: lambda i, h: normalise(i, h, K0, n0, x0),
                    RELU0: lambda i, h: relu_t(i, h, K0),
                    NORM2: lambda i, h: normalise(i, h, K2B, n2, u),
                    NORMH: lambda i, h: normalise(i, h, KH, n0, u),
                    Y: y_t,
                    EXPZ: exp_z,
                    NORM3: lambda i, h: normalise(i, h, K3, n2, x3),
                    RELU3: lambda i, h: relu_t(i, h, K3),
                })

            @block.gpsimd
            def _(g):
                root_chain = [Chain(g, pool_chain[h], 5) for h in range(H)]

                def inverse_root(i, h, k):
                    ch = root_chain[h]
                    if k == K0:
                        ch.start(i)
                    ch.goes_on(i)
                    g.wait_ge(var_ready[k], i * H + h + 1)
                    ch.link(g.tensor_tensor(small[h][:, RSTD, :], small[h][:, VAR, :], half[:, :], ALU.pow))
                    g.tensor_tensor(small[h][:, NB, :], small[h][:, NMEAN, :], small[h][:, RSTD, :],
                                    ALU.mult).then_inc(rstd_ready[k], 1)
                    if k == K3:
                        ch.end()

                def wide(t):
                    return t[:, :].rearrange("p (o c) -> p o c", o=1).to_broadcast([P, W, C])

                def add_b1(i, h):
                    g.wait_ge(x1_ready, i * H + h + 1)
                    g.tensor_tensor(x2[h][:, :, :], x1[h][:, :, :], wide(b1rows), ALU.add).then_inc(x2_ready, 1)

                def form_h2(i, h):
                    g.wait_ge(rows_ready[K2B], i * H + h + 1)
                    root_chain[h].goes_on(i)
                    root_chain[h].link(g.tensor_tensor(u[h][:, :, :], n2[h][:, :, :], wide(g1rows), ALU.mult))
                    g.tensor_tensor(u[h][:, :, :], u[h][:, :, :], wide(hrrows), ALU.add).then_inc(h2_ready, 1)

                def add_w(i, h):
                    g.wait_ge(w_ready, i * H + h + 1)
                    g.tensor_tensor(x3[h][:, :, :], x3[h][:, :, :], x1[h][:, :, :], ALU.add).then_inc(x3_ready, 1)

                pipeline(g, H, STEPS, nodes, {
                    ROOT0: lambda i, h: inverse_root(i, h, K0),
                    X2: add_b1,
                    ROOT2: lambda i, h: inverse_root(i, h, K2B),
                    H2: form_h2,
                    ROOTH: lambda i, h: inverse_root(i, h, KH),
                    X3SUM: add_w,
                    ROOT3: lambda i, h: inverse_root(i, h, K3),
                })

            @block.tensor
            def _(pe):
                def transposes(i, h, k, src):
                    at = i * H + h + 1
                    pe.wait_ge(rows_ready[k], at)
                    wait(pe, *{K0: (out_ready, at - H), KH: (x1_ready, at), K3: (w_ready, at)}[k])
                    for w in range(W):
                        ins = pe.transpose(tile(h, w), src[h][:, w, :], ident[:, :])
                    ins.then_inc(t_ready[k], 1)

                def product(i, h, k, weight, bias=None):
                    pe.wait_ge(hT_ready[k], i * H + h + 1)
                    if k == KH:
                        pe.wait_ge(y_used, i * H + h + 1)
                    for w in range(W):
                        ins = pe.matmul(tile(h, w), hT[h][:, w, :], weight[:, :], start=True, stop=bias is None)
                        if bias is not None:
                            ins = pe.matmul(tile(h, w), ones3[:, :], bias[:, :], start=False, stop=True)
                    ins.then_inc(mm_ready[k], 1)

                def y_rows(i, h):
                    pe.wait_ge(hT_ready[KH], i * H + h + 1)
                    for w in range(W):
                        ins = pe.transpose(tile(h, w), hT[h][:, w, :], ident[:, :])
                    ins.then_inc(y_ready, 1)

                pipeline(pe, H, STEPS, nodes, {
                    TURN0: lambda i, h: transposes(i, h, K0, n0),
                    RES0: lambda i, h: product(i, h, K0, wres0),
                    TURNH: lambda i, h: transposes(i, h, KH, n0),
                    Y: y_rows,
                    Z: lambda i, h: product(i, h, KH, wsi, biassi),
                    TURN3: lambda i, h: transposes(i, h, K3, n2),
                    OUT3: lambda i, h: product(i, h, K3, w3, bias3),
                })

            @block.vector
            def _(v):
                chains = [Chain(v, dve_chain[h], 5 * 4 + 1) for h in range(H)]

                def stats(i, h, k, src):
                    ch, sm = chains[h], small[h]
                    ch.goes_on(i)
                    for w in range(W):
                        ins = v.bn_stats(st[h][:, w, :], src[h][:, w, :])
                    ch.link(ins)
                    even, odd = st[h][:, :, 1:3], st[h][:, :, 4:6]
                    v.tensor_tensor(sm[:, DIF, :], even[:, :, 0], odd[:, :, 0], ALU.subtract)
                    v.tensor_tensor(sm[:, M2, :], even[:, :, 1], odd[:, :, 1], ALU.add)
                    ch.link(v.tensor_tensor(sm[:, SUM, :], even[:, :, 0], odd[:, :, 0], ALU.add))
                    v.tensor_scalar(sm[:, NMEAN, :], sm[:, SUM, :], -0.5, None, ALU.mult)
                    ch.link(v.scalar_tensor_tensor(out=sm[:, DIF, :], in0=sm[:, DIF, :], scalar=0.25,
                                                   in1=sm[:, DIF, :], op0=ALU.mult, op1=ALU.mult))
                    ch.link(v.scalar_tensor_tensor(out=sm[:, VAR, :], in0=sm[:, M2, :], scalar=1.0 / C,
                                                   in1=sm[:, DIF, :], op0=ALU.mult, op1=ALU.add))
                    if k == K2B:
                        ins = v.tensor_tensor(sm[:, VAR, :], sm[:, VAR, :], sm[:, EPS2, :], ALU.add)
                    else:
                        ins = v.tensor_scalar(sm[:, VAR, :], sm[:, VAR, :], EPS, None, ALU.add)
                    ins.then_inc(var_ready[k], 1)

                def stats0(i, h):
                    chains[h].start(i)
                    v.wait_ge(x_loaded[h], 16 * (i + 1))
                    wait(v, rows_ready[K3], (i - 1) * H + h + 1)
                    stats(i, h, K0, x0)

                def form_x1(i, h):
                    at = i * H + h + 1
                    v.wait_ge(mm_ready[K0], at)
                    wait(v, x1_stored[h], 16 * i)
                    wait(v, x3_ready, at - H)
                    v.tensor_tensor(flat(x1[h]), bk(h), flat(x0[h]), ALU.add).then_inc(x1_ready, 1)

                def stats2(i, h):
                    at = i * H + h + 1
                    v.wait_ge(x2_ready, at)
                    v.wait_ge(rows_ready[K0], at)
                    stats(i, h, K2A, x2)
                    v.wait_ge(var_ready[K2A], at)
                    v.tensor_scalar(small[h][:, EPS2, :], small[h][:, VAR, :], EPS, None, ALU.mult)
                    for w in range(W):
                        ins = v.tensor_scalar(u[h][:, w, :], x2[h][:, w, :], small[h][:, NMEAN, w:w + 1], 0.0,
                                              ALU.add, ALU.max)
                    chains[h].link(ins)
                    stats(i, h, K2B, u)

                def stats_h(i, h):
                    v.wait_ge(h2_ready, i * H + h + 1)
                    stats(i, h, KH, u)

                def form_x3(i, h):
                    v.wait_ge(y_ready, i * H + h + 1)
                    wait(v, out_stored[h], 16 * i)
                    v.scalar_tensor_tensor(out=flat(x3[h]), in0=bk(h), scalar=-1.0, in1=flat(x2[h]),
                                           op0=ALU.add, op1=ALU.add).then_inc(y_used, 1)

                def elu(i, h):
                    v.wait_ge(exp_ready, i * H + h + 1)
                    v.wait_ge(x1_stored[h], 16 * (i + 1))
                    v.scalar_tensor_tensor(out=flat(x1[h]), in0=flat(u[h]), scalar=1.0, in1=bk(h),
                                           op0=ALU.min, op1=ALU.max).then_inc(w_ready, 1)

                def stats3(i, h):
                    v.wait_ge(x3_ready, i * H + h + 1)
                    stats(i, h, K3, x3)

                def form_out(i, h):
                    v.wait_ge(mm_ready[K3], i * H + h + 1)
                    v.wait_ge(rows_ready[K3], i * H + h + 1)
                    v.scalar_tensor_tensor(out=flat(x3[h]), in0=bk(h), scalar=0.0, in1=flat(x3[h]),
                                           op0=ALU.max, op1=ALU.add).then_inc(out_ready, 1)
                    chains[h].end()

                pipeline(v, H, STEPS, nodes, {
                    STATS0: stats0, X1: form_x1, STATS2: stats2, STATSH: stats_h, X3: form_x3, ELU: elu,
                    STATS3: stats3, OUT: form_out,
                })

        SUM, DIF, M2, NMEAN, VAR, EPS2, RSTD, NB = range(8)

        def row_stats(v, ch, st, sm, src, tiles, add_eps, signal):
            for w in range(tiles):
                ins = v.bn_stats(st[:, w, :], src[:, w, :])
            ch.link(ins)
            even, odd = st[:, 0:tiles, 1:3], st[:, 0:tiles, 4:6]
            t = slice(0, tiles)
            v.tensor_tensor(sm[:, DIF, t], even[:, :, 0], odd[:, :, 0], ALU.subtract)
            v.tensor_tensor(sm[:, M2, t], even[:, :, 1], odd[:, :, 1], ALU.add)
            ch.link(v.tensor_tensor(sm[:, SUM, t], even[:, :, 0], odd[:, :, 0], ALU.add))
            v.tensor_scalar(sm[:, NMEAN, t], sm[:, SUM, t], -0.5, None, ALU.mult)
            ch.link(v.scalar_tensor_tensor(out=sm[:, DIF, t], in0=sm[:, DIF, t], scalar=0.25, in1=sm[:, DIF, t],
                                           op0=ALU.mult, op1=ALU.mult))
            ch.link(v.scalar_tensor_tensor(out=sm[:, VAR, t], in0=sm[:, M2, t], scalar=1.0 / C, in1=sm[:, DIF, t],
                                           op0=ALU.mult, op1=ALU.add))
            if add_eps:
                ins = v.tensor_scalar(sm[:, VAR, t], sm[:, VAR, t], EPS, None, ALU.add)
            else:
                ins = v.tensor_tensor(sm[:, VAR, t], sm[:, VAR, t], sm[:, EPS2, t], ALU.add)
            ins.then_inc(signal, 1)

        def inverse_root(g, link, at, sm, tiles, ready, signal, factor=None):
            t = slice(0, tiles)
            g.wait_ge(ready, at)
            g.tensor_tensor(sm[:, RSTD, t], sm[:, VAR, t], half[:, t], ALU.pow).then_inc(link, 1)
            steps = 1 if factor is None else 2
            if factor is not None:
                g.wait_ge(link, (at - 1) * steps + 1)
                g.tensor_tensor(sm[:, RSTD, t], sm[:, RSTD, t], factor, ALU.mult).then_inc(link, 1)
            g.wait_ge(link, (at - 1) * steps + steps)
            g.tensor_tensor(sm[:, NB, t], sm[:, NMEAN, t], sm[:, RSTD, t], ALU.mult).then_inc(signal, 1)

        def normalise(act, at, sm, dst, src, tiles, ready, signal):
            act.wait_ge(ready, at)
            for w in range(tiles):
                ins = act.activation(dst[:, w, :], src[:, w, :], ACT.Identity, scale=sm[:, RSTD, w:w + 1],
                                     bias=sm[:, NB, w:w + 1])
            ins.then_inc(signal, 1)

        def group_rows(t, g):
            width = t.shape[1]
            return t.rearrange("e c -> (e c)")[bass.ds(g * EG * width, EG * width)].rearrange(
                "(w p c) -> p w c", w=EW, p=P)

        def mask_row(k, g):
            return masks[k][bass.ds(g * EG, EG)].rearrange("(o e) -> o e", o=1).to_broadcast([P, EG])

        def ebank(h, k):
            return bank(h // 2, 2 * (h % 2) + k)

        def etile(h, k, w, rows=P):
            return ps[h // 2][0:rows, 1024 * (h % 2) + 512 * k + w * C:1024 * (h % 2) + 512 * k + (w + 1) * C]

        def stage(g, table, dst, at, staged, passed, free=()):
            for sem_, value in free:
                wait(g, sem_, value)
            g.sem_inc(passed, 1)
            g.tensor_copy(dst, table[:, bass.ds((at - 1) * EW, EW)]).then_inc(staged, 1)

        def gather(g, dst, table, index, signal, limit):
            for w in range(EW):
                g.indirect_dma_start(out=dst[:, w, :], out_offset=None, in_=table,
                                     in_offset=bass.IndirectOffsetOnAxis(ap=index[:, w:w + 1], axis=0),
                                     bounds_check=limit, oob_is_err=False).then_inc(signal, 16)

        def scatter(g, table, src, index, signal, limit):
            for w in range(EW):
                g.indirect_dma_start(out=table, out_offset=bass.IndirectOffsetOnAxis(ap=index[:, w:w + 1], axis=0),
                                     in_=src[:, w, :], in_offset=None,
                                     bounds_check=limit, oob_is_err=False).then_inc(signal, 16)

        def softmax_scans(v, ch, h, g, m, z, r, e, ab, neg, m_done):
            before = (h - 1) % U
            if not isinstance(g, int) or g:
                v.wait_ge(m_done, g)
                ch.link(v.tensor_copy(m[h][:, 0:1], m[before][:, EG:EG + 1]))
            else:
                ch.link(v.memset(m[h][:, 0:1], NEG))
            v.tensor_tensor_scan(m[h][:, 1:EG + 1], neg[h][:, :], e[h][:, :], m[h][:, 0:1], ALU.add, ALU.max
                                 ).then_inc(m_done, 1)
            v.wait_ge(m_done, g + 1)
            v.tensor_tensor(ab[h][:, 1, :], e[h][:, :], m[h][:, 1:EG + 1], ALU.subtract)
            ch.link(v.tensor_tensor(ab[h][:, 0, :], m[h][:, 0:EG], neg[h][:, :], ALU.add))

        def last_of(buf, h, g):
            return 0.0 if isinstance(g, int) and g == 0 else buf[(h - 1) % U][:, EG - 1:EG]

        with Phase(nc) as phase, ExitStack() as ctx:
            def sem(name):
                return phase.semaphore("l0_" + name)

            def bufs(name, shape, dt=F32):
                return [sb(f"l0_{name}{h}", shape, dt, ctx) for h in range(U)]

            def sems(name):
                return [sem(f"{name}{h}") for h in range(U)]

            xin = bufs("xin", [P, 2 * EW, C])
            nrm = bufs("nrm", [P, 2 * EW, C])
            hT = bufs("hT", [P, 2, EG])
            q = bufs("q", [P, EG])
            kq = bufs("kq", [P, EG])
            e = bufs("e", [P, EG])
            neg = bufs("neg", [P, EG])
            m = bufs("m", [P, EG + 1])
            z = bufs("z", [P, EG])
            r = bufs("r", [P, EG])
            ab = bufs("ab", [P, 2, EG])
            xo = bufs("xo", [P, EW, C])
            st = bufs("st", [P, 2 * EW, 6])
            small = bufs("small", [P, 8, 2 * EW])
            index = bufs("index", [P, 3, EW], I32)
            gathered, stored, scattered, neg_in = sems("gathered"), sems("stored"), sems("scattered"), sems("neg_in")
            chains = sems("dve_chain")
            (staged, passed, var_ready, root_link, rstd_ready, rows_ready, t_ready, hT_ready, kq_ready, q_ready,
             prod_ready, ev_ready, e_ready, m_done, ab_ready, exp_ready, z_done, r_done, rst_ready, sum_ready,
             x1_ready, scat_staged) = [sem(n) for n in (
                 "staged", "passed", "var_ready", "root_link", "rstd_ready", "rows_ready", "t_ready", "hT_ready",
                 "kq_ready", "q_ready", "prod_ready", "ev_ready", "e_ready", "m_done", "ab_ready", "exp_ready",
                 "z_done", "r_done", "rst_ready", "sum_ready", "x1_ready", "scat_staged")]
            block = ctx.enter_context(nc.Block())
            (GATHER, STATS, ROOT, NORM, TURN, RELU, KQ, Q, PROD, EV, ESC, MAXI, EXPO, SUMS, RES, X1, PUT,
             STEPS) = range(18)

            @block.sync
            def _(sp):
                def load(i, h):
                    wait(sp, ab_ready, (i - 1) * U + h + 1)
                    sp.dma_start(neg[h][:, :], mask_row(1, i * U + h)).then_inc(neg_in[h], 16)

                def store(i, h):
                    sp.wait_ge(x1_ready, i * U + h + 1)
                    sp.dma_start(group_rows(x1_e, i * U + h), xo[h][:, :, :]).then_inc(stored[h], 16)

                pipeline(sp, U, STEPS, groups, {STATS: load, PUT: store})
                for h in range(U):
                    sp.wait_ge(stored[h], 16 * (groups // U))

            @block.gpsimd
            def _(g):
                limit = g.to_reg(N - 1)

                def fetch(i, h):
                    at = i * U + h + 1
                    stage(g, src_i, index[h][:, 0, :], at, staged, passed, [(x1_ready, at - U)])
                    g.tensor_copy(index[h][:, 1, :], dst_i[:, bass.ds((at - 1) * EW, EW)]).then_inc(staged, 1)
                    g.wait_ge(staged, 2 * at)
                    g.sem_inc(passed, 1)
                    gather(g, xin[h][:, 0:EW, :], a["x"], index[h][:, 0, :], gathered[h], limit)
                    gather(g, xin[h][:, EW:2 * EW, :], a["x"], index[h][:, 1, :], gathered[h], limit)

                def put(i, h):
                    at = i * U + h + 1
                    stage(g, scat_i, index[h][:, 2, :], at, scat_staged, passed, [(x1_ready, at)])
                    g.wait_ge(scat_staged, at)
                    g.sem_inc(passed, 1)
                    scatter(g, t_x1, xo[h], index[h][:, 2, :], scattered[h], limit)

                pipeline(g, U, STEPS, groups, {
                    GATHER: fetch,
                    ROOT: lambda i, h: inverse_root(g, root_link, i * U + h + 1, small[h], 2 * EW, var_ready,
                                                    rstd_ready),
                    PUT: put,
                })
                for h in range(U):
                    g.wait_ge(scattered[h], 16 * EW * (groups // U))

            @block.scalar
            def _(act):
                def norm(i, h):
                    at = i * U + h + 1
                    wait(act, t_ready, at - U)
                    normalise(act, at, small[h], nrm[h], xin[h], 2 * EW, rstd_ready, rows_ready)

                def relu_t(i, h):
                    at = i * U + h + 1
                    act.wait_ge(t_ready, at)
                    wait(act, sum_ready, at - U)
                    act.activation(hT[h][:, :, :], ps[h // 2][:, 1024 * (h % 2):1024 * (h % 2) + 1024].rearrange(
                        "p (k c) -> p k c", k=2), ACT.Relu).then_inc(hT_ready, 1)

                def copy_q(i, h):
                    at = i * U + h + 1
                    act.wait_ge(kq_ready, at)
                    wait(act, prod_ready, at - U)
                    act.activation(q[h][:, :], ebank(h, 1), ACT.Identity).then_inc(q_ready, 1)

                def copy_e(i, h):
                    at = i * U + h + 1
                    act.wait_ge(ev_ready, at)
                    wait(act, rst_ready, at - U)
                    act.activation(e[h][:, :], ebank(h, 1), ACT.Identity).then_inc(e_ready, 1)

                def exps(i, h):
                    act.wait_ge(ab_ready, i * U + h + 1)
                    act.activation(ab[h][:, :, :], ab[h][:, :, :], ACT.Exp).then_inc(exp_ready, 1)

                pipeline(act, U, STEPS, groups, {NORM: norm, RELU: relu_t, Q: copy_q, ESC: copy_e, EXPO: exps})

            @block.tensor
            def _(pe):
                def turn_rows(i, h):
                    at = i * U + h + 1
                    pe.wait_ge(rows_ready, at)
                    wait(pe, x1_ready, at - U)
                    for w in range(2 * EW):
                        ins = pe.transpose(etile(h, w // EW, w % EW), nrm[h][:, w, :], ident[:, :])
                    ins.then_inc(t_ready, 1)

                def k_and_q(i, h):
                    pe.wait_ge(hT_ready, i * U + h + 1)
                    pe.matmul(ebank(h, 0), wqkv[:, 1, :], hT[h][:, 0, :], start=True, stop=True)
                    pe.matmul(ebank(h, 1), wqkv[:, 0, :], hT[h][:, 1, :], start=True, stop=True).then_inc(kq_ready, 1)

                def e_and_v(i, h):
                    at = i * U + h + 1
                    pe.wait_ge(prod_ready, at)
                    pe.matmul(ebank(h, 1), heads[:, :], kq[h][:, :], start=True, stop=True)
                    pe.matmul(ebank(h, 0), wqkv[:, 2, :], hT[h][:, 0, :], start=True, stop=True).then_inc(ev_ready, 1)

                def sums(i, h):
                    at = i * U + h + 1
                    pe.wait_ge(rst_ready, at)
                    for w in range(EW):
                        t = slice(w * C, (w + 1) * C)
                        pe.matmul(etile(h, 1, w), hT[h][:, 1, t], wres0[:, :], start=True, stop=False)
                        ins = pe.matmul(etile(h, 1, w), r[h][:, t], ident[:, :], start=False, stop=True)
                    ins.then_inc(sum_ready, 1)

                pipeline(pe, U, STEPS, groups, {TURN: turn_rows, KQ: k_and_q, EV: e_and_v, RES: sums})

            @block.vector
            def _(v):
                ch = [Chain(v, chains[h], 9) for h in range(U)]

                def stats(i, h):
                    ch[h].start(i)
                    v.wait_ge(gathered[h], 16 * 2 * EW * (i + 1))
                    wait(v, rows_ready, (i - 1) * U + h + 1)
                    row_stats(v, ch[h], st[h], small[h], xin[h], 2 * EW, True, var_ready)

                def product(i, h):
                    at = i * U + h + 1
                    v.wait_ge(q_ready, at)
                    v.tensor_tensor(kq[h][:, :], ebank(h, 0), q[h][:, :], ALU.mult).then_inc(prod_ready, 1)

                def maxima(i, h):
                    at = i * U + h + 1
                    ch[h].goes_on(i)
                    v.wait_ge(e_ready, at)
                    v.wait_ge(neg_in[h], 16 * (i + 1))
                    ch[h].link(v.scalar_tensor_tensor(out=e[h][:, :], in0=e[h][:, :], scalar=SLOPE, in1=e[h][:, :],
                                                      op0=ALU.mult, op1=ALU.max))
                    softmax_scans(v, ch[h], h, i * U + h, m, z, r, e, ab, neg, m_done)
                    v.tensor_tensor(ab[h][:, 0, :], ab[h][:, 0, :], m[h][:, 1:EG + 1], ALU.subtract
                                    ).then_inc(ab_ready, 1)

                def weighted(i, h):
                    at = i * U + h + 1
                    g = i * U + h
                    ch[h].goes_on(i)
                    v.wait_ge(exp_ready, at)
                    wait(v, z_done, g)
                    v.tensor_tensor_scan(z[h][:, :], ab[h][:, 0, :], ab[h][:, 1, :], last_of(z, h, g), ALU.mult,
                                         ALU.add).then_inc(z_done, 1)
                    v.wait_ge(ev_ready, at)
                    ch[h].link(v.tensor_tensor(ab[h][:, 1, :], ebank(h, 0), ab[h][:, 1, :], ALU.mult))
                    wait(v, r_done, g)
                    wait(v, sum_ready, at - U)
                    v.tensor_tensor_scan(kq[h][:, :], ab[h][:, 0, :], ab[h][:, 1, :], last_of(kq, h, g), ALU.mult,
                                         ALU.add).then_inc(r_done, 1)
                    v.wait_ge(z_done, at)
                    ch[h].link(v.reciprocal(e[h][:, :], z[h][:, :]))
                    v.wait_ge(r_done, at)
                    v.tensor_tensor(r[h][:, :], kq[h][:, :], e[h][:, :], ALU.mult).then_inc(rst_ready, 1)

                def form_x1(i, h):
                    at = i * U + h + 1
                    v.wait_ge(sum_ready, at)
                    wait(v, stored[h], 16 * i)
                    wait(v, scattered[h], 16 * EW * i)
                    v.tensor_tensor(flat(xo[h]), ebank(h, 1), flat(xin[h][:, EW:2 * EW, :]), ALU.add
                                    ).then_inc(x1_ready, 1)
                    ch[h].goes_on(i)
                    ch[h].end()

                pipeline(v, U, STEPS, groups, {STATS: stats, PROD: product, MAXI: maxima, SUMS: weighted,
                                               X1: form_x1})

        with Phase(nc) as phase, ExitStack() as ctx:
            def sem(name):
                return phase.semaphore("l1_" + name)

            def bufs(name, shape, dt=F32):
                return [sb(f"l1_{name}{h}", shape, dt, ctx) for h in range(U)]

            def sems(name):
                return [sem(f"{name}{h}") for h in range(U)]

            xin = bufs("xin", [P, EW, C])
            xe = bufs("xe", [P, EW, C])
            nrm = bufs("nrm", [P, EW, C])
            hT = bufs("hT", [P, EG])
            attr = bufs("attr", [P, EW, 16])
            attrT = bufs("attrT", [16, EG])
            ew = bufs("ew", [P, EG])
            msg = bufs("msg", [P, EG])
            agg = bufs("agg", [P, EG])
            same = bufs("same", [P, EG])
            x2 = bufs("x2", [P, EW, C])
            u = bufs("u", [P, EW, C])
            n2 = bufs("n2", [P, EW, C])
            st = bufs("st", [P, EW, 6])
            small = bufs("small", [P, 8, EW])
            index = bufs("index", [P, 2, EW], I32)
            gathered, stored, scattered, loaded, chains = (sems(n) for n in (
                "gathered", "stored", "scattered", "loaded", "dve_chain"))
            (staged, passed, var_ready, root_link, rstd_ready, rows_ready, t_ready, hT_ready, prod_ready, ew_ready,
             agg_done, agg_ready, back_ready, x2_ready, var2a, var2_ready, root2_link, rstd2_ready, n2_ready,
             scat_staged) = [sem(n) for n in (
                 "staged", "passed", "var_ready", "root_link", "rstd_ready", "rows_ready", "t_ready", "hT_ready",
                 "prod_ready", "ew_ready", "agg_done", "agg_ready", "back_ready", "x2_ready", "var2a", "var2_ready",
                 "root2_link", "rstd2_ready", "n2_ready", "scat_staged")]
            block = ctx.enter_context(nc.Block())
            (GATHER, STATS, ROOT, NORM, TURN, RELU, XW, EWC, AGG, AGGB, BACK, X2, NORMS2, ROOT2, N2, PUT,
             STEPS) = range(17)

            @block.sync
            def _(sp):
                def load(i, h):
                    g = i * U + h
                    wait(sp, x2_ready, g + 1 - U)
                    sp.dma_start(xe[h][:, :, :], group_rows(x1_e, g)).then_inc(loaded[h], 16)
                    sp.dma_start(attr[h][:, :, :], group_rows(attr_e, g)).then_inc(loaded[h], 16)
                    sp.dma_start(same[h][:, :], mask_row(0, g)).then_inc(loaded[h], 16)

                def store(i, h):
                    sp.wait_ge(x2_ready, i * U + h + 1)
                    sp.dma_start(group_rows(x2_e, i * U + h), x2[h][:, :, :]).then_inc(stored[h], 16)

                pipeline(sp, U, STEPS, groups, {GATHER: load, X2: store})
                for h in range(U):
                    sp.wait_ge(stored[h], 16 * (groups // U))

            @block.gpsimd
            def _(g):
                limit = g.to_reg(N - 1)

                def fetch(i, h):
                    at = i * U + h + 1
                    stage(g, src_i, index[h][:, 0, :], at, staged, passed, [(rows_ready, at - U)])
                    g.wait_ge(staged, at)
                    g.sem_inc(passed, 1)
                    gather(g, xin[h], t_x1, index[h][:, 0, :], gathered[h], limit)

                def put(i, h):
                    at = i * U + h + 1
                    stage(g, scat_i, index[h][:, 1, :], at, scat_staged, passed, [(n2_ready, at)])
                    g.wait_ge(scat_staged, at)
                    g.sem_inc(passed, 1)
                    scatter(g, t_n2, n2[h], index[h][:, 1, :], scattered[h], limit)

                pipeline(g, U, STEPS, groups, {
                    GATHER: fetch,
                    ROOT: lambda i, h: inverse_root(g, root_link, i * U + h + 1, small[h], EW, var_ready, rstd_ready),
                    ROOT2: lambda i, h: inverse_root(g, root2_link, i * U + h + 1, small[h], EW, var2_ready,
                                                     rstd2_ready),
                    PUT: put,
                })
                for h in range(U):
                    g.wait_ge(scattered[h], 16 * EW * (groups // U))

            @block.scalar
            def _(act):
                def norm(i, h):
                    at = i * U + h + 1
                    wait(act, t_ready, at - U)
                    normalise(act, at, small[h], nrm[h], xin[h], EW, rstd_ready, rows_ready)

                def relu_t(i, h):
                    at = i * U + h + 1
                    act.wait_ge(t_ready, at)
                    wait(act, prod_ready, at - U)
                    act.activation(hT[h][:, :], ebank(h, 0), ACT.Relu)
                    act.activation(attrT[h][:, :], ebank(h, 1)[0:16, :], ACT.Identity).then_inc(hT_ready, 1)

                def copy_ew(i, h):
                    at = i * U + h + 1
                    act.wait_ge(prod_ready, at)
                    wait(act, back_ready, at - U)
                    act.activation(ew[h][:, :], ebank(h, 1), ACT.Identity).then_inc(ew_ready, 1)

                def add_b(i, h):
                    at = i * U + h + 1
                    act.wait_ge(agg_done, at)
                    act.activation(ew[h][:, :], agg[h][:, :], ACT.Identity, bias=col(B1)).then_inc(agg_ready, 1)

                def norm2(i, h):
                    at = i * U + h + 1
                    wait(act, scattered[h], 16 * EW * i)
                    normalise(act, at, small[h], n2[h], u[h], EW, rstd2_ready, n2_ready)

                pipeline(act, U, STEPS, groups, {NORM: norm, RELU: relu_t, EWC: copy_ew, AGGB: add_b, N2: norm2})

            @block.tensor
            def _(pe):
                def turn_rows(i, h):
                    at = i * U + h + 1
                    pe.wait_ge(rows_ready, at)
                    pe.wait_ge(loaded[h], 48 * (i + 1))
                    wait(pe, x2_ready, at - U)
                    for w in range(EW):
                        pe.transpose(etile(h, 0, w), nrm[h][:, w, :], ident[:, :])
                        ins = pe.transpose(etile(h, 1, w, 16), attr[h][:, w, :], ident[:, :])
                    ins.then_inc(t_ready, 1)

                def products(i, h):
                    pe.wait_ge(hT_ready, i * U + h + 1)
                    pe.matmul(ebank(h, 0), w1[:, :], hT[h][:, :], start=True, stop=True)
                    pe.matmul(ebank(h, 1), edge_w[:, :], attrT[h][:, :], start=True, stop=True).then_inc(prod_ready, 1)

                def back(i, h):
                    pe.wait_ge(agg_ready, i * U + h + 1)
                    for w in range(EW):
                        ins = pe.transpose(etile(h, 0, w), ew[h][:, w * C:(w + 1) * C], ident[:, :])
                    ins.then_inc(back_ready, 1)

                pipeline(pe, U, STEPS, groups, {TURN: turn_rows, XW: products, BACK: back})

            @block.vector
            def _(v):
                ch = [Chain(v, chains[h], 14) for h in range(U)]

                def stats(i, h):
                    ch[h].start(i)
                    v.wait_ge(gathered[h], 16 * EW * (i + 1))
                    wait(v, n2_ready, (i - 1) * U + h + 1)
                    row_stats(v, ch[h], st[h], small[h], xin[h], EW, True, var_ready)

                def aggregate(i, h):
                    at, g = i * U + h + 1, i * U + h
                    ch[h].goes_on(i)
                    v.wait_ge(ew_ready, at)
                    ch[h].link(v.tensor_tensor(msg[h][:, :], ebank(h, 0), ew[h][:, :], ALU.mult))
                    v.wait_ge(loaded[h], 48 * (i + 1))
                    wait(v, agg_done, g)
                    wait(v, agg_ready, at - U)
                    v.tensor_tensor_scan(agg[h][:, :], same[h][:, :], msg[h][:, :], last_of(agg, h, g), ALU.mult,
                                         ALU.add).then_inc(agg_done, 1)

                def form_x2(i, h):
                    at = i * U + h + 1
                    v.wait_ge(back_ready, at)
                    v.wait_ge(loaded[h], 48 * (i + 1))
                    wait(v, stored[h], 16 * i)
                    v.tensor_tensor(flat(x2[h]), ebank(h, 0), flat(xe[h]), ALU.add).then_inc(x2_ready, 1)

                def norms2(i, h):
                    at = i * U + h + 1
                    ch[h].goes_on(i)
                    v.wait_ge(x2_ready, at)
                    v.wait_ge(rows_ready, at)
                    row_stats(v, ch[h], st[h], small[h], x2[h], EW, True, var2a)
                    v.wait_ge(var2a, at)
                    v.tensor_scalar(small[h][:, EPS2, :], small[h][:, VAR, :], EPS, None, ALU.mult)
                    for w in range(EW):
                        ins = v.tensor_scalar(u[h][:, w, :], x2[h][:, w, :], small[h][:, NMEAN, w:w + 1], 0.0, ALU.add,
                                              ALU.max)
                    ch[h].link(ins)
                    row_stats(v, ch[h], st[h], small[h], u[h], EW, False, var2_ready)
                    ch[h].end()

                pipeline(v, U, STEPS, groups, {STATS: stats, AGG: aggregate, X2: form_x2, NORMS2: norms2})

        with Phase(nc) as phase, ExitStack() as ctx:
            def sem(name):
                return phase.semaphore("l2_" + name)

            def bufs(name, shape, dt=F32):
                return [sb(f"l2_{name}{h}", shape, dt, ctx) for h in range(U)]

            def sems(name):
                return [sem(f"{name}{h}") for h in range(U)]

            xin = bufs("xin", [P, 2 * EW, C])
            hT = bufs("hT", [P, 2, EG])
            fs = bufs("fs", [P, EG])
            fd = bufs("fd", [P, EG])
            e = bufs("e", [P, EG])
            pool = bufs("pool", [P, EG])
            pm = bufs("pm", [P, EG])
            neg = bufs("neg", [P, EG])
            m = bufs("m", [P, EG + 1])
            z = bufs("z", [P, EG])
            r = bufs("r", [P, EG])
            ab = bufs("ab", [P, 2, EG])
            gf = bufs("gf", [64, EG])
            xe = bufs("xe", [P, EW, C])
            h2 = bufs("h2", [P, EW, C])
            x3 = bufs("x3", [P, EW, C])
            n3 = bufs("n3", [P, EW, C])
            st = bufs("st", [P, EW, 6])
            small = bufs("small", [P, 8, EW])
            index = bufs("index", [P, 3, EW], I32)
            gathered, stored, scattered, loaded, chains = (sems(n) for n in (
                "gathered", "stored", "scattered", "loaded", "dve_chain"))
            (staged, passed, t_ready, hT_ready, f_ready, fc_ready, prod_ready, ep_ready, e_ready, m_done, pm_done,
             ab_ready, exp_ready, z_done, r_done, agg_ready, gf_ready, gfc_ready, gate_ready, ex_ready, att_ready,
             h2_sum, h2_ready, varh_ready, rooth_link, rstdh_ready, nh_ready, th_ready, yT_ready, y_ready, y_used,
             zz_ready, ez_ready, w_done, x3_ready, var3_ready, root3_link, rstd3_ready, n3_ready, scat_staged) = [
                 sem(n) for n in (
                     "staged", "passed", "t_ready", "hT_ready", "f_ready", "fc_ready", "prod_ready", "ep_ready",
                     "e_ready", "m_done", "pm_done", "ab_ready", "exp_ready", "z_done", "r_done", "agg_ready",
                     "gf_ready", "gfc_ready", "gate_ready", "ex_ready", "att_ready", "h2_sum", "h2_ready",
                     "varh_ready", "rooth_link", "rstdh_ready", "nh_ready", "th_ready", "yT_ready", "y_ready",
                     "y_used", "zz_ready", "ez_ready", "w_done", "x3_ready", "var3_ready", "root3_link",
                     "rstd3_ready", "n3_ready", "scat_staged")]
            block = ctx.enter_context(nc.Block())
            (GATHER, TURN, GAIN, FEAT, FC, PROD, EP, EC, MAXI, EXPO, SUMS, GF, GFC, GATE, EX, ATT, HSUM, HC, STATSH,
             ROOTH, NH, TH, YT, Y, X3, ZZ, EZ, ELU, STATS3, ROOT3, N3, PUT, STEPS) = range(33)

            @block.sync
            def _(sp):
                def load(i, h):
                    g = i * U + h
                    wait(sp, x3_ready, g + 1 - U)
                    sp.dma_start(xe[h][:, :, :], group_rows(x2_e, g)).then_inc(loaded[h], 16)
                    sp.dma_start(neg[h][:, :], mask_row(1, g)).then_inc(loaded[h], 16)

                def store_x3(i, h):
                    sp.wait_ge(x3_ready, i * U + h + 1)
                    sp.dma_start(group_rows(x3_e, i * U + h), x3[h][:, :, :]).then_inc(stored[h], 16)

                def store_n3(i, h):
                    sp.wait_ge(n3_ready, i * U + h + 1)
                    sp.dma_start(group_rows(n3_e, i * U + h), n3[h][:, :, :]).then_inc(stored[h], 16)

                pipeline(sp, U, STEPS, groups, {GATHER: load, STATS3: store_x3, PUT: store_n3})
                for h in range(U):
                    sp.wait_ge(stored[h], 32 * (groups // U))

            @block.gpsimd
            def _(g):
                limit = g.to_reg(N - 1)

                def fetch(i, h):
                    at = i * U + h + 1
                    stage(g, src_i, index[h][:, 0, :], at, staged, passed, [(t_ready, at - U)])
                    g.tensor_copy(index[h][:, 1, :], dst_i[:, bass.ds((at - 1) * EW, EW)]).then_inc(staged, 1)
                    g.wait_ge(staged, 2 * at)
                    g.sem_inc(passed, 1)
                    gather(g, xin[h][:, 0:EW, :], t_n2, index[h][:, 0, :], gathered[h], limit)
                    gather(g, xin[h][:, EW:2 * EW, :], t_n2, index[h][:, 1, :], gathered[h], limit)

                def put(i, h):
                    at = i * U + h + 1
                    stage(g, scat_i, index[h][:, 2, :], at, scat_staged, passed, [(n3_ready, at)])
                    g.wait_ge(scat_staged, at)
                    g.sem_inc(passed, 1)
                    scatter(g, t_n3, n3[h], index[h][:, 2, :], scattered[h], limit)

                pipeline(g, U, STEPS, groups, {
                    GATHER: fetch,
                    ROOTH: lambda i, h: inverse_root(g, rooth_link, i * U + h + 1, small[h], EW, varh_ready,
                                                     rstdh_ready),
                    ROOT3: lambda i, h: inverse_root(g, root3_link, i * U + h + 1, small[h], EW, var3_ready,
                                                     rstd3_ready, dinv[:, bass.ds((i * U + h) * EW, EW)]),
                    PUT: put,
                })
                for h in range(U):
                    g.wait_ge(scattered[h], 16 * EW * (groups // U))

            @block.scalar
            def _(act):
                def gain(i, h):
                    at = i * U + h + 1
                    act.wait_ge(t_ready, at)
                    wait(act, h2_sum, at - U)
                    act.activation(hT[h][:, :, :], ps[h // 2][:, 1024 * (h % 2):1024 * (h % 2) + 1024].rearrange(
                        "p (k c) -> p k c", k=2), ACT.Identity, scale=col(G1), bias=col(S1)).then_inc(hT_ready, 1)

                def copy_f(i, h):
                    at = i * U + h + 1
                    act.wait_ge(f_ready, at)
                    wait(act, h2_sum, at - U)
                    act.activation(fs[h][:, :], ebank(h, 0), ACT.Identity)
                    act.activation(fd[h][:, :], ebank(h, 1), ACT.Identity).then_inc(fc_ready, 1)

                def copy_e(i, h):
                    at = i * U + h + 1
                    act.wait_ge(ep_ready, at)
                    wait(act, att_ready, at - U)
                    act.activation(e[h][:, :], ebank(h, 0), ACT.Identity, scale=1.0 / DH ** 0.5)
                    act.activation(pool[h][:, :], ebank(h, 1), ACT.Relu, bias=col(BPOOL)).then_inc(e_ready, 1)

                def exps(i, h):
                    act.wait_ge(ab_ready, i * U + h + 1)
                    act.activation(ab[h][:, :, :], ab[h][:, :, :], ACT.Exp).then_inc(exp_ready, 1)

                def gate_bias(i, h):
                    at = i * U + h + 1
                    act.wait_ge(gf_ready, at)
                    wait(act, gate_ready, at - U)
                    act.activation(gf[h][:, :], ebank(h, 0)[0:64, :], ACT.Identity, bias=bgate[:, :]
                                   ).then_inc(gfc_ready, 1)

                def gate_exp(i, h):
                    at = i * U + h + 1
                    act.wait_ge(gate_ready, at)
                    act.wait_ge(agg_ready, at)
                    act.activation(ab[h][:, 0, :], ebank(h, 1), ACT.Exp, scale=-1.0, bias=col(NBGR))
                    act.activation(ab[h][:, 1, :], fd[h][:, :], ACT.Exp).then_inc(ex_ready, 1)

                def copy_h2(i, h):
                    at = i * U + h + 1
                    act.wait_ge(h2_sum, at)
                    wait(act, w_done, at - U)
                    act.activation(flat(h2[h]), ebank(h, 0), ACT.Identity).then_inc(h2_ready, 1)

                def norm_h(i, h):
                    at = i * U + h + 1
                    wait(act, stored[h], 32 * i)
                    wait(act, scattered[h], 16 * EW * i)
                    normalise(act, at, small[h], n3[h], h2[h], EW, rstdh_ready, nh_ready)

                def y_t(i, h):
                    at = i * U + h + 1
                    act.wait_ge(th_ready, at)
                    act.activation(pool[h][:, :], ebank(h, 0), ACT.Identity, scale=col(G2), bias=col(S2)
                                   ).then_inc(yT_ready, 1)

                def exp_z(i, h):
                    act.wait_ge(zz_ready, i * U + h + 1)
                    act.activation(flat(h2[h]), ebank(h, 0), ACT.Exp, bias=-1.0).then_inc(ez_ready, 1)

                def norm3(i, h):
                    at = i * U + h + 1
                    act.wait_ge(th_ready, at)
                    normalise(act, at, small[h], n3[h], x3[h], EW, rstd3_ready, n3_ready)

                pipeline(act, U, STEPS, groups, {GAIN: gain, FC: copy_f, EC: copy_e, EXPO: exps, GFC: gate_bias,
                                                 EX: gate_exp, HC: copy_h2, NH: norm_h, YT: y_t, EZ: exp_z,
                                                 N3: norm3})

            @block.tensor
            def _(pe):
                def turn_rows(i, h):
                    at = i * U + h + 1
                    pe.wait_ge(gathered[h], 16 * 2 * EW * (i + 1))
                    wait(pe, w_done, at - U)
                    for w in range(2 * EW):
                        ins = pe.transpose(etile(h, w // EW, w % EW), xin[h][:, w, :], ident[:, :])
                    ins.then_inc(t_ready, 1)

                def features(i, h):
                    pe.wait_ge(hT_ready, i * U + h + 1)
                    pe.matmul(ebank(h, 0), wattn[:, :], hT[h][:, 0, :], start=True, stop=True)
                    pe.matmul(ebank(h, 1), wattn[:, :], hT[h][:, 1, :], start=True, stop=True).then_inc(f_ready, 1)

                def e_and_pool(i, h):
                    pe.wait_ge(prod_ready, i * U + h + 1)
                    pe.matmul(ebank(h, 0), heads[:, :], e[h][:, :], start=True, stop=True)
                    pe.matmul(ebank(h, 1), wpool[:, :], hT[h][:, 0, :], start=True, stop=True).then_inc(ep_ready, 1)

                def gate_features(i, h):
                    at = i * U + h + 1
                    pe.wait_ge(pm_done, at)
                    pe.wait_ge(e_ready, at)
                    pe.matmul(ebank(h, 0)[0:64, :], wgself[:, :], hT[h][:, 1, :], start=True, stop=False)
                    pe.matmul(ebank(h, 0)[0:64, :], wgneigh[:, :], pm[h][:, :], start=False, stop=True
                              ).then_inc(gf_ready, 1)

                def gate(i, h):
                    pe.wait_ge(gfc_ready, i * U + h + 1)
                    pe.matmul(ebank(h, 1), wgr[:, :], gf[h][:, :], start=True, stop=True).then_inc(gate_ready, 1)

                def h2_rows(i, h):
                    pe.wait_ge(att_ready, i * U + h + 1)
                    for w in range(EW):
                        t = slice(w * C, (w + 1) * C)
                        pe.matmul(etile(h, 0, w), fd[h][:, t], whr[:, :], start=True, stop=False)
                        pe.matmul(etile(h, 0, w), hT[h][:, 1, t], ident[:, :], start=False, stop=False)
                        ins = pe.matmul(etile(h, 0, w), ones3[:, :], biashr[:, :], start=False, stop=True)
                    ins.then_inc(h2_sum, 1)

                def turn_h(i, h):
                    at = i * U + h + 1
                    pe.wait_ge(nh_ready, at)
                    for w in range(EW):
                        ins = pe.transpose(etile(h, 0, w), n3[h][:, w, :], ident[:, :])
                    ins.then_inc(th_ready, 1)

                def y_rows(i, h):
                    pe.wait_ge(yT_ready, i * U + h + 1)
                    for w in range(EW):
                        ins = pe.transpose(etile(h, 1, w), pool[h][:, w * C:(w + 1) * C], ident[:, :])
                    ins.then_inc(y_ready, 1)

                def z_rows(i, h):
                    pe.wait_ge(yT_ready, i * U + h + 1)
                    for w in range(EW):
                        pe.matmul(etile(h, 0, w), pool[h][:, w * C:(w + 1) * C], wsi[:, :], start=True, stop=False)
                        ins = pe.matmul(etile(h, 0, w), ones3[:, :], biassi[:, :], start=False, stop=True)
                    ins.then_inc(zz_ready, 1)

                pipeline(pe, U, STEPS, groups, {TURN: turn_rows, FEAT: features, EP: e_and_pool, GF: gate_features,
                                                GATE: gate, HSUM: h2_rows, TH: turn_h, Y: y_rows, ZZ: z_rows})

            @block.vector
            def _(v):
                ch = [Chain(v, chains[h], 16) for h in range(U)]

                def product(i, h):
                    at = i * U + h + 1
                    ch[h].start(i)
                    v.wait_ge(fc_ready, at)
                    wait(v, att_ready, at - U)
                    v.tensor_tensor(e[h][:, :], fs[h][:, :], fd[h][:, :], ALU.mult).then_inc(prod_ready, 1)

                def maxima(i, h):
                    at, g = i * U + h + 1, i * U + h
                    ch[h].goes_on(i)
                    v.wait_ge(e_ready, at)
                    v.wait_ge(loaded[h], 32 * (i + 1))
                    softmax_scans(v, ch[h], h, g, m, z, r, e, ab, neg, m_done)
                    v.tensor_tensor(ab[h][:, 0, :], ab[h][:, 0, :], m[h][:, 1:EG + 1], ALU.subtract
                                    ).then_inc(ab_ready, 1)
                    wait(v, pm_done, g)
                    wait(v, gf_ready, at - U)
                    first = NEG if isinstance(g, int) and g == 0 else pm[(h - 1) % U][:, EG - 1:EG]
                    v.tensor_tensor_scan(pm[h][:, :], neg[h][:, :], pool[h][:, :], first, ALU.add, ALU.max
                                         ).then_inc(pm_done, 1)

                def weighted(i, h):
                    at, g = i * U + h + 1, i * U + h
                    ch[h].goes_on(i)
                    v.wait_ge(exp_ready, at)
                    wait(v, z_done, g)
                    v.tensor_tensor_scan(z[h][:, :], ab[h][:, 0, :], ab[h][:, 1, :], last_of(z, h, g), ALU.mult,
                                         ALU.add).then_inc(z_done, 1)
                    ch[h].link(v.tensor_tensor(fs[h][:, :], fs[h][:, :], ab[h][:, 1, :], ALU.mult))
                    wait(v, r_done, g)
                    v.tensor_tensor_scan(r[h][:, :], ab[h][:, 0, :], fs[h][:, :], last_of(r, h, g), ALU.mult,
                                         ALU.add).then_inc(r_done, 1)
                    v.wait_ge(z_done, at)
                    ch[h].link(v.reciprocal(e[h][:, :], z[h][:, :]))
                    v.wait_ge(r_done, at)
                    v.tensor_tensor(fd[h][:, :], r[h][:, :], e[h][:, :], ALU.mult).then_inc(agg_ready, 1)

                def attention(i, h):
                    at = i * U + h + 1
                    ch[h].goes_on(i)
                    v.wait_ge(ex_ready, at)
                    ch[h].mark(v.tensor_scalar(ab[h][:, 1, :], ab[h][:, 1, :], 1.0, -1.0, ALU.min, ALU.add))
                    ch[h].link(v.tensor_scalar(ab[h][:, 0, :], ab[h][:, 0, :], 1.0, None, ALU.add))
                    ch[h].mark(v.reciprocal(e[h][:, :], ab[h][:, 0, :]))
                    ch[h].link(v.tensor_tensor(fd[h][:, :], fd[h][:, :], ab[h][:, 1, :], ALU.max))
                    v.tensor_tensor(fd[h][:, :], fd[h][:, :], e[h][:, :], ALU.mult).then_inc(att_ready, 1)

                def stats_h(i, h):
                    ch[h].goes_on(i)
                    v.wait_ge(h2_ready, i * U + h + 1)
                    wait(v, n3_ready, (i - 1) * U + h + 1)
                    row_stats(v, ch[h], st[h], small[h], h2[h], EW, True, varh_ready)

                def form_x3(i, h):
                    at = i * U + h + 1
                    v.wait_ge(y_ready, at)
                    v.wait_ge(loaded[h], 32 * (i + 1))
                    wait(v, stored[h], 32 * i)
                    v.scalar_tensor_tensor(out=flat(x3[h]), in0=ebank(h, 1), scalar=-1.0, in1=flat(xe[h]), op0=ALU.add,
                                           op1=ALU.add).then_inc(y_used, 1)

                def elu(i, h):
                    at = i * U + h + 1
                    v.wait_ge(ez_ready, at)
                    v.scalar_tensor_tensor(out=e[h][:, :], in0=flat(h2[h]), scalar=1.0, in1=ebank(h, 0), op0=ALU.min,
                                           op1=ALU.max).then_inc(w_done, 1)
                    v.wait_ge(w_done, at)
                    v.wait_ge(y_used, at)
                    v.tensor_tensor(flat(x3[h]), flat(x3[h]), e[h][:, :], ALU.add).then_inc(x3_ready, 1)

                def stats3(i, h):
                    ch[h].goes_on(i)
                    v.wait_ge(x3_ready, i * U + h + 1)
                    v.wait_ge(nh_ready, i * U + h + 1)
                    row_stats(v, ch[h], st[h], small[h], x3[h], EW, True, var3_ready)
                    ch[h].end()

                pipeline(v, U, STEPS, groups, {PROD: product, MAXI: maxima, SUMS: weighted, ATT: attention,
                                               STATSH: stats_h, X3: form_x3, ELU: elu, STATS3: stats3})

        with Phase(nc) as phase, ExitStack() as ctx:
            def sem(name):
                return phase.semaphore("l3_" + name)

            def bufs(name, shape, dt=F32):
                return [sb(f"l3_{name}{h}", shape, dt, ctx) for h in range(U)]

            def sems(name):
                return [sem(f"{name}{h}") for h in range(U)]

            xin = bufs("xin", [P, EW, C])
            own = bufs("own", [P, EW, C])
            hT = bufs("hT", [P, 2, EG])
            agg = bufs("agg", [P, EG])
            total = bufs("total", [P, EG])
            same = bufs("same", [P, EG])
            xe = bufs("xe", [P, EW, C])
            scaled = bufs("scaled", [P, EW, C])
            res = bufs("res", [P, EW, C])
            factor = bufs("factor", [P, EW])
            index = bufs("index", [P, 2, EW], I32)
            gathered, scattered, loaded = (sems(n) for n in ("gathered", "scattered", "loaded"))
            (staged, passed, t_ready, hT_ready, agg_done, total_ready, mm_ready, scaled_ready, out_ready,
             scat_staged) = [sem(n) for n in (
                 "staged", "passed", "t_ready", "hT_ready", "agg_done", "total_ready", "mm_ready", "scaled_ready",
                 "out_ready", "scat_staged")]
            factor_ready = sem("factor_ready")
            block = ctx.enter_context(nc.Block())
            GATHER, TURN, RELU, AGG, MM, OUT, PUT, STEPS = range(8)

            @block.sync
            def _(sp):
                def load(i, h):
                    g = i * U + h
                    wait(sp, out_ready, g + 1 - U)
                    sp.dma_start(own[h][:, :, :], group_rows(n3_e, g)).then_inc(loaded[h], 16)
                    sp.dma_start(xe[h][:, :, :], group_rows(x3_e, g)).then_inc(loaded[h], 16)
                    sp.dma_start(same[h][:, :], mask_row(0, g)).then_inc(loaded[h], 16)

                pipeline(sp, U, STEPS, groups, {GATHER: load})

            @block.gpsimd
            def _(g):
                limit = g.to_reg(N - 1)

                def fetch(i, h):
                    at = i * U + h + 1
                    stage(g, src_i, index[h][:, 0, :], at, staged, passed, [(t_ready, at - U)])
                    g.wait_ge(staged, at)
                    g.sem_inc(passed, 1)
                    gather(g, xin[h], t_n3, index[h][:, 0, :], gathered[h], limit)

                def put(i, h):
                    at = i * U + h + 1
                    stage(g, scat_i, index[h][:, 1, :], at, scat_staged, passed, [(out_ready, at)])
                    g.wait_ge(scat_staged, at)
                    g.sem_inc(passed, 1)
                    scatter(g, out, res[h], index[h][:, 1, :], scattered[h], limit)

                pipeline(g, U, STEPS, groups, {GATHER: fetch, PUT: put})
                for h in range(U):
                    g.wait_ge(scattered[h], 16 * EW * (groups // U))

            @block.scalar
            def _(act):
                def relu_t(i, h):
                    at = i * U + h + 1
                    act.wait_ge(t_ready, at)
                    wait(act, total_ready, at - U)
                    act.activation(hT[h][:, :, :], ps[h // 2][:, 1024 * (h % 2):1024 * (h % 2) + 1024].rearrange(
                        "p (k c) -> p k c", k=2), ACT.Relu).then_inc(hT_ready, 1)

                pipeline(act, U, STEPS, groups, {RELU: relu_t})

            @block.tensor
            def _(pe):
                def turn_rows(i, h):
                    at = i * U + h + 1
                    pe.wait_ge(gathered[h], 16 * EW * (i + 1))
                    pe.wait_ge(loaded[h], 48 * (i + 1))
                    wait(pe, out_ready, at - U)
                    for w in range(EW):
                        pe.transpose(etile(h, 0, w), xin[h][:, w, :], ident[:, :])
                        ins = pe.transpose(etile(h, 1, w), own[h][:, w, :], ident[:, :])
                    ins.then_inc(t_ready, 1)

                def product(i, h):
                    pe.wait_ge(total_ready, i * U + h + 1)
                    for w in range(EW):
                        ins = pe.matmul(etile(h, 0, w), total[h][:, w * C:(w + 1) * C], w3[:, :], start=True,
                                        stop=True)
                    ins.then_inc(mm_ready, 1)

                pipeline(pe, U, STEPS, groups, {TURN: turn_rows, MM: product})

            @block.vector
            def _(v):
                def aggregate(i, h):
                    at, g = i * U + h + 1, i * U + h
                    v.wait_ge(hT_ready, at)
                    v.wait_ge(loaded[h], 48 * (i + 1))
                    wait(v, agg_done, g)
                    v.tensor_tensor_scan(agg[h][:, :], same[h][:, :], hT[h][:, 0, :], last_of(agg, h, g), ALU.mult,
                                         ALU.add).then_inc(agg_done, 1)
                    v.wait_ge(agg_done, at)
                    wait(v, mm_ready, at - U)
                    v.tensor_tensor(total[h][:, :], agg[h][:, :], hT[h][:, 1, :], ALU.add).then_inc(total_ready, 1)

                def form_out(i, h):
                    at = i * U + h + 1
                    v.wait_ge(mm_ready, at)
                    v.tensor_copy(factor[h][:, :], dinv[:, bass.ds((at - 1) * EW, EW)]).then_inc(factor_ready, 1)
                    v.wait_ge(factor_ready, at)
                    for w in range(EW):
                        ins = v.scalar_tensor_tensor(out=scaled[h][:, w, :], in0=etile(h, 0, w),
                                                     scalar=factor[h][:, w:w + 1], in1=b3rows[:, :], op0=ALU.mult,
                                                     op1=ALU.add)
                    ins.then_inc(scaled_ready, 1)
                    v.wait_ge(scaled_ready, at)
                    wait(v, scattered[h], 16 * EW * i)
                    v.scalar_tensor_tensor(out=flat(res[h]), in0=flat(scaled[h]), scalar=0.0, in1=flat(xe[h]),
                                           op0=ALU.max, op1=ALU.add).then_inc(out_ready, 1)

                pipeline(v, U, STEPS, groups, {AGG: aggregate, OUT: form_out})


_INS = ['x', 'src', 'dst', 'edge_attr_16', 'L0_gnn_Wq', 'L0_gnn_Wk', 'L0_gnn_Wv', 'L0_gnn_Wres', 'L1_gnn_W',
        'L1_gnn_edge_w', 'L1_gnn_b', 'L2_gnn_ln1_g', 'L2_gnn_ln1_b', 'L2_gnn_W_attn', 'L2_gnn_W_pool',
        'L2_gnn_b_pool', 'L2_gnn_W_gself', 'L2_gnn_W_gneigh', 'L2_gnn_b_gate', 'L2_gnn_W_gr', 'L2_gnn_b_gr',
        'L2_gnn_W_hr', 'L2_gnn_b_hr', 'L2_gnn_ln2_g', 'L2_gnn_ln2_b', 'L2_gnn_W_si', 'L2_gnn_b_si', 'L3_gnn_W',
        'L3_gnn_b']


def kernel(**inputs):
    import numpy as _np
    import concourse.bacc as _bacc
    from concourse import mybir as _mybir
    from concourse.bass_utils import run_bass_kernel_spmd as _run

    nc = _bacc.Bacc("TRN2", target_bir_lowering=False, num_devices=1)
    arrays, args = {}, {}
    for name in _INS:
        v = _np.ascontiguousarray(inputs[name])
        arrays[f"in_{name}_dram"] = v
        args[name] = nc.dram_tensor(f"in_{name}_dram", v.shape, _mybir.dt.from_np(v.dtype), kind="ExternalInput").ap()
    out = nc.dram_tensor("out_0_dram", inputs["x"].shape, _mybir.dt.float32, kind="ExternalOutput").ap()
    bass_gnn(nc, args, out)
    r = _run(nc, [arrays], core_ids=[0])
    return r.results[0]["out_0_dram"]
```

```python
from contextlib import ExitStack

import concourse.bass as bass
from concourse import mybir

P = 128
C = 128
W = 8
H = 4
EW = 4
EG = EW * P
U = 4
DH = 16
SLOPE = 0.2
EPS = 1e-5
NEG = -1.0e30
BIG = float(1 << 22)

ALU = mybir.AluOpType
ACT = mybir.ActivationFunctionType
AX = mybir.AxisListType
F32 = mybir.dt.float32
BF16 = mybir.dt.bfloat16
I32 = mybir.dt.int32


class Chain:

    def __init__(self, eng, sem, steps, at=1):
        self.eng, self.sem, self.steps, self.before, self.n = eng, sem, steps, (at - 1) * steps, 0

    def mark(self, ins):
        ins.then_inc(self.sem, 1)
        self.n += 1
        return self.n

    def wait(self, n=None):
        self.eng.wait_ge(self.sem, self.before + (n or self.n))

    def link(self, ins):
        self.mark(ins)
        self.wait()

    def end(self):
        assert self.n == self.steps, (self.n, self.steps)


class Phase:

    def __init__(self, nc):
        self.nc, self.semaphores = nc, []

    def semaphore(self, name):
        self.semaphores.append(self.nc.alloc_semaphore(name=name))
        return self.semaphores[-1]

    def __enter__(self):
        return self

    def __exit__(self, *error):
        if error[0] is None:
            self.nc.clear_and_free_semaphores(self.semaphores)
            self.nc.all_engine_barrier()


def wait(eng, sem, value):
    if not isinstance(value, int) or value > 0:
        eng.wait_ge(sem, value)


def pipeline(eng, lanes, begins, total, work):
    count = -(-total // lanes)
    order = sorted(work, key=lambda step: begins[step] % 1)

    def turn(i):
        for h in range(lanes):
            for step in order:
                k = h - int(begins[step])
                at, lane = i + k // lanes, k % lanes
                if not isinstance(i, int) or 0 <= at and at * lanes + lane < total:
                    work[step](at, lane)

    for i in range(3):
        turn(i)
    with eng.Fori(3, count - 1) as i:
        turn(i)
    for i in range(count - 1, count + 2):
        turn(i)


def flat(t):
    return t.rearrange("p w c -> p (w c)")


def bass_gnn(nc, a, out):
    N = a["x"].shape[0]
    E = a["src"].shape[0]
    GN = P * W
    nodes = -(-N // GN)
    groups = -(-E // EG)
    EP = groups * EG
    T = EP // P
    L = EP // P

    def dram(name, shape, dt=F32):
        return nc.dram_tensor(name, shape, dt).ap()

    t_x1 = dram("t_x1", [N, C])
    t_n2 = dram("t_n2", [N, C])
    t_n3 = dram("t_n3", [N, C])
    x1_e = dram("x1_e", [EP, C])
    x2_e = dram("x2_e", [EP, C])
    x3_e = dram("x3_e", [EP, C])
    n3_e = dram("n3_e", [EP, C])
    attr_e = dram("attr_e", [EP, 16])
    masks = dram("masks", [2, EP])
    lin = dram("lin", [4, EP])

    with ExitStack() as top:
        def sb(name, shape, dt=F32, ctx=top):
            return ctx.enter_context(nc.sbuf_tensor(name, shape, dt))

        ident = sb("ident", [P, P])
        heads = sb("heads", [P, P])
        wqkv = sb("wqkv", [P, 3, C])
        wres0 = sb("wres0", [P, C])
        w1 = sb("w1", [P, C])
        edge_w = sb("edge_w", [16, C])
        wattn = sb("wattn", [P, C])
        wpool = sb("wpool", [P, C])
        wgself = sb("wgself", [P, 64])
        wgneigh = sb("wgneigh", [P, 64])
        wgr = sb("wgr", [64, C])
        whr = sb("whr", [P, C])
        wsi = sb("wsi", [P, C])
        w3 = sb("w3", [P, C])
        ones3 = sb("ones3", [3, P], BF16)
        bias1 = sb("bias1", [3, C], BF16)
        bias3 = sb("bias3", [3, C], BF16)
        biassi = sb("biassi", [3, C], BF16)
        biashr = sb("biashr", [3, C], BF16)
        b3rows = sb("b3rows", [P, C])
        cols = sb("cols", [P, 8])
        G1, S1, G2, S2, BPOOL, HBGR = range(6)
        b1rows = sb("b1rows", [P, C])
        g1rows = sb("g1rows", [P, C])
        hrrows = sb("hrrows", [P, C])
        bgate = sb("bgate", [64, 1])
        half = sb("half", [P, 2 * EW])
        src_i = sb("src_i", [P, T], I32)
        dst_i = sb("dst_i", [P, T], I32)
        scat_i = sb("scat_i", [P, T], I32)
        dinv = sb("dinv", [P, T])
        ps = [top.enter_context(nc.psum_tensor(f"ps{h}", [P, 4 * 512], F32)) for h in range(2)]

        def bank(h, k, n=1):
            return ps[h][:, 512 * k:512 * (k + n)]

        def col(k, p=P):
            return cols[0:p, k:k + 1]

        with Phase(nc) as phase, ExitStack() as ctx:
            def sem(name):
                return phase.semaphore(name)

            raw = sb("raw", [P, 4, C], F32, ctx)
            rows = sb("bias_rows", [1, 4, C], F32, ctx)
            part = sb("bias_part", [1, 4, 3, C], BF16, ctx)
            left = sb("bias_left", [1, 4, C], F32, ctx)
            wgr8 = sb("wgr8", [64, 8], F32, ctx)
            bgr8 = sb("bgr8", [8, 1], F32, ctx)
            head8 = sb("head8", [8, P], F32, ctx)
            hrrows2 = sb("hrrows2", [P, C], F32, ctx)
            ints = sb("ints", [P, 4, L], I32, ctx)
            val = sb("val", [P, 4, L], F32, ctx)
            same = sb("same", [P, L], F32, ctx)
            more = sb("more", [P, L], F32, ctx)
            one = sb("one", [P, L], F32, ctx)
            halfl = sb("halfl", [P, L], F32, ctx)
            count = sb("count", [P, L], F32, ctx)
            mask2 = sb("mask2", [P, 2, L], F32, ctx)
            tabs = sb("tabs", [P, 4, L], F32, ctx)
            ends = sb("ends", [P, 2], F32, ctx)
            line = sb("line", [1, 4, P], F32, ctx)
            carry = sb("carry", [P, 1], F32, ctx)
            back = sb("back", [T // 2, 4, 2, P], F32, ctx)
            loaded, edges_in, filled, spread = sem("loaded"), sem("edges_in"), sem("filled"), sem("spread")
            tabled, reloaded, pool_ok, pe_ok = sem("tabled"), sem("reloaded"), sem("pool_ok"), sem("pe_ok")
            parts_ready, ends_ready, line_ready = sem("parts_ready"), sem("ends_ready"), sem("line_ready")
            count_ready, dinv_ready, link = sem("count_ready"), sem("dinv_ready"), sem("link")
            block = ctx.enter_context(nc.Block())
            FULL, REST = E // L, E % L
            blank = sb("blank", [P, (EP - E) * 16 // P], F32, ctx)
            blanked, attr_in = sem("blanked"), sem("attr_in")
            assert (EP - E) * 16 % P == 0

            loads = [(raw[:, k, :], a["L0_gnn_" + n]) for k, n in enumerate(("Wq", "Wk", "Wv", "Wres"))]
            loads += [(w1[:, :], a["L1_gnn_W"]), (edge_w[:, :], a["L1_gnn_edge_w"]),
                      (wattn[:, :], a["L2_gnn_W_attn"]), (wpool[:, :], a["L2_gnn_W_pool"]),
                      (wgself[:, :], a["L2_gnn_W_gself"]), (wgneigh[:, :], a["L2_gnn_W_gneigh"]),
                      (wgr8[:, :], a["L2_gnn_W_gr"]), (whr[:, :], a["L2_gnn_W_hr"]), (wsi[:, :], a["L2_gnn_W_si"]),
                      (w3[:, :], a["L3_gnn_W"])]
            loads += [(rows[:, k, :], a[n].rearrange("(o c) -> o c", o=1))
                      for k, n in enumerate(("L3_gnn_b", "L2_gnn_b_si", "L2_gnn_b_hr", "L1_gnn_b"))]
            loads += [(t[:, :], a[n].rearrange("(o c) -> o c", o=1).to_broadcast([P, C])) for t, n in (
                (b3rows, "L3_gnn_b"), (b1rows, "L1_gnn_b"), (g1rows, "L2_gnn_ln1_g"), (hrrows, "L2_gnn_ln1_b"),
                (hrrows2, "L2_gnn_b_hr"))]
            loads += [(d, a[n].rearrange("(c o) -> c o", o=1)) for d, n in (
                (col(G1), "L2_gnn_ln1_g"), (col(S1), "L2_gnn_ln1_b"),
                (col(G2), "L2_gnn_ln2_g"), (col(S2), "L2_gnn_ln2_b"), (col(BPOOL), "L2_gnn_b_pool"),
                (bgate[:, :], "L2_gnn_b_gate"), (bgr8[:, :], "L2_gnn_b_gr"))]
            nload = len(loads)

            def edge_loads():
                d, s = a["dst"], a["src"]
                for k, t in ((0, d), (3, s)):
                    yield ints[0:FULL, k, :], t[0:FULL * L].rearrange("(p l) -> p l", l=L)
                    if REST:
                        yield ints[FULL:FULL + 1, k, 0:REST], t[FULL * L:E].rearrange("(o l) -> o l", o=1)
                yield ints[0:1, 1, 1:L], d[0:L - 1].rearrange("(o l) -> o l", o=1)
                yield ints[1:FULL, 1, :], d[L - 1:FULL * L - 1].rearrange("(p l) -> p l", l=L)
                yield ints[FULL:FULL + 1, 1, 0:REST], d[FULL * L - 1:E - 1].rearrange("(o l) -> o l", o=1)
                yield ints[0:FULL, 2, :], d[1:FULL * L + 1].rearrange("(p l) -> p l", l=L)
                yield ints[FULL:FULL + 1, 2, 0:REST - 1], d[FULL * L + 1:E].rearrange("(o l) -> o l", o=1)

            edge_list = list(edge_loads())

            @block.sync
            def _(sp):
                sp.wait_ge(filled, 4)
                sp.dma_start(attr_e[0:E, :], a["edge_attr_16"]).then_inc(attr_in, 16)
                sp.wait_ge(blanked, 1)
                sp.dma_start(attr_e[E:EP, :].rearrange("e c -> (e c)").rearrange("(p k) -> p k", p=P), blank[:, :]
                             ).then_inc(attr_in, 16)
                for dst, src in edge_list:
                    sp.dma_start(dst, src).then_inc(edges_in, 16)
                with nc.allow_non_contiguous_dma(reason="a few columns of weights' length"):
                    for dst, src in loads:
                        sp.dma_start(dst, src).then_inc(loaded, 16)
                sp.wait_ge(parts_ready, 1)
                for k, dst in enumerate((bias3, biassi, biashr, bias1)):
                    for j in range(3):
                        sp.dma_start(dst[j:j + 1, :], part[:, k, j, :]).then_inc(spread, 16)
                sp.wait_ge(count_ready, 1)
                sp.wait_ge(dinv_ready, 1)
                for k in range(2):
                    sp.dma_start(masks[k].rearrange("(p l) -> p l", p=P), mask2[:, k, :]).then_inc(tabled, 16)
                for k in range(4):
                    sp.dma_start(lin[k].rearrange("(p l) -> p l", p=P), tabs[:, k, :]).then_inc(tabled, 16)
                sp.wait_ge(tabled, 16 * 6)
                for k in range(4):
                    for j in range(2):
                        sp.dma_start(back[:, k, j, :],
                                     lin[k].rearrange("(j t p) -> j t p", j=2, p=P)[j]).then_inc(reloaded, 16)
                sp.wait_ge(attr_in, 32)
                sp.wait_ge(spread, 16 * 12)
                sp.wait_ge(reloaded, 16 * 8)

            @block.gpsimd
            def _(g):
                g.memset(ident[:, :], 0.0).then_inc(pool_ok, 1)
                g.memset(heads[:, :], 1.0).then_inc(pool_ok, 1)
                g.memset(head8[:, :], 1.0).then_inc(pool_ok, 1)
                g.memset(half[:, :], -0.5).then_inc(pool_ok, 1)
                g.memset(halfl[:, :], -0.5).then_inc(pool_ok, 1)
                g.wait_ge(pool_ok, 5)
                g.affine_select(out=ident[:, :], in_=ident[:, :], compare_op=ALU.not_equal, fill=1.0, base=0,
                                pattern=[[-1, P]], channel_multiplier=1).then_inc(pool_ok, 1)

                def in_head(t, first, sign, wait_for):
                    g.wait_ge(pool_ok, wait_for)
                    v = t[:, :].rearrange("p (h d) -> p h d", d=DH)
                    step, inner, mult = first
                    base = 0 if sign > 0 else DH - 1
                    g.affine_select(out=v, in_=v, compare_op=ALU.is_ge, fill=0.0, base=base,
                                    pattern=[[sign * step, P // DH], [sign * inner, DH]],
                                    channel_multiplier=sign * mult).then_inc(pool_ok, 1)
                in_head(heads, (-DH, 0, 1), 1, 6)
                in_head(heads, (-DH, 0, 1), -1, 7)
                in_head(head8, (DH, 1, -DH), 1, 8)
                in_head(head8, (DH, 1, -DH), -1, 9)
                g.wait_ge(count_ready, 1)
                g.tensor_tensor(tabs[:, 3, :], count[:, :], halfl[:, :], ALU.pow).then_inc(dinv_ready, 1)

            @block.tensor
            def _(pe):
                pe.wait_ge(pool_ok, 10)
                pe.wait_ge(loaded, 16 * nload)
                for k in range(4):
                    ins = pe.transpose(ps[0][:, k * C:(k + 1) * C], raw[:, k, :], ident[:, :])
                ins.then_inc(pe_ok, 1)
                pe.matmul(ps[1][:, 0:1], head8[:, :], bgr8[:, :], start=True, stop=True).then_inc(pe_ok, 1)
                pe.wait_ge(ends_ready, 1)
                pe.transpose(ps[1][0:1, 512:512 + P], ends[:, 0:1], ident[:, :])
                pe.transpose(ps[1][0:1, 512 + P:512 + 2 * P], ends[:, 1:2], ident[:, :]).then_inc(pe_ok, 1)
                pe.wait_ge(line_ready, 1)
                pe.transpose(ps[1][:, 1024:1025], line[0:1, 3, :], ident[0:1, 0:1]).then_inc(pe_ok, 1)
                pe.wait_ge(reloaded, 16 * 8)
                for k in range(4):
                    for j in range(2):
                        o = 256 * k + (T // 2) * j
                        ins = pe.transpose(ps[0][:, 1024 + o:1024 + o + T // 2], back[:, k, j, :],
                                           ident[0:T // 2, 0:T // 2])
                ins.then_inc(pe_ok, 1)

            @block.vector
            def _(v):
                ch = Chain(v, link, 35)
                v.memset(blank[:, :], 0.0).then_inc(blanked, 1)
                for k, value in ((0, N), (1, -1), (2, -1), (3, 0)):
                    v.memset(ints[:, k, :], value).then_inc(filled, 1)
                ch.mark(v.memset(one[:, :], 1.0))
                ch.mark(v.memset(ones3[:, :], 1.0))
                ch.mark(v.memset(line[:, :, :], 0.0))
                v.wait_ge(edges_in, 16 * len(edge_list))
                v.wait_ge(filled, 4)
                ch.link(v.tensor_copy(val[:, :, :], ints[:, :, :]))
                ch.mark(v.tensor_tensor(same[:, :], val[:, 0, :], val[:, 1, :], ALU.is_equal))
                ch.link(v.tensor_tensor(more[:, :], val[:, 0, :], val[:, 2, :], ALU.is_equal))
                ch.mark(v.tensor_tensor_scan(count[:, :], same[:, :], one[:, :], 0.0, ALU.mult, ALU.add))
                ch.mark(v.tensor_reduce(ends[:, 1:2], same[:, :], AX.X, ALU.min))
                ch.wait()
                ch.link(v.tensor_copy(ends[:, 0:1], count[:, L - 1:L]))
                v.sem_inc(ends_ready, 1)
                v.wait_ge(loaded, 16 * nload)
                ch.mark(v.tensor_copy(left[:, 0, :], rows[:, 0, :]))
                ch.mark(v.tensor_copy(left[:, 2:4, :], rows[:, 2:4, :]))
                ch.link(v.tensor_scalar(left[:, 1, :], rows[:, 1, :], 1.0, None, ALU.add))
                for j in range(3):
                    ch.link(v.tensor_copy(part[:, :, j, :], left[:, :, :]))
                    if j < 2:
                        ch.link(v.tensor_tensor(left[:, :, :], left[:, :, :], part[:, :, j, :], ALU.subtract))
                v.sem_inc(parts_ready, 1)
                ch.mark(v.scalar_tensor_tensor(out=tabs[:, 2, :], in0=more[:, :], scalar=BIG, in1=val[:, 0, :],
                                               op0=ALU.mult, op1=ALU.add))
                ch.mark(v.tensor_copy(tabs[:, 0, :], val[:, 3, :]))
                ch.mark(v.tensor_copy(tabs[:, 1, :], val[:, 0, :]))
                ch.mark(v.tensor_copy(mask2[:, 0, :], same[:, :]))
                ch.link(v.tensor_scalar(mask2[:, 1, :], same[:, :], 1.0, -NEG, ALU.subtract, ALU.mult))
                v.wait_ge(pe_ok, 3)
                ch.link(v.tensor_copy(line[:, 0:2, :], ps[1][0:1, 512:512 + 2 * P].rearrange("p (k c) -> p k c", k=2)))
                ch.link(v.tensor_tensor_scan(line[:, 2, :], line[:, 1, :], line[:, 0, :], 0.0, ALU.mult, ALU.add))
                ch.link(v.tensor_copy(line[:, 3, 1:P], line[:, 2, 0:P - 1]))
                v.sem_inc(line_ready, 1)
                v.wait_ge(pe_ok, 4)
                ch.link(v.tensor_copy(carry[:, :], ps[1][:, 1024:1025]))
                ch.link(v.tensor_tensor_scan(count[:, :], same[:, :], one[:, :], carry[:, :], ALU.mult, ALU.add))
                ch.link(v.tensor_scalar(count[:, :], count[:, :], 1.0, None, ALU.add))
                v.sem_inc(count_ready, 1)
                v.tensor_copy(wqkv[:, :, :], ps[0][:, 0:3 * C].rearrange("p (k c) -> p k c", k=3))
                v.tensor_copy(wres0[:, :], ps[0][:, 3 * C:4 * C])
                v.tensor_scalar(col(HBGR), ps[1][:, 0:1], 0.5, None, ALU.mult)
                v.tensor_scalar(whr[:, :], whr[:, :], 0.5, None, ALU.mult)
                v.tensor_copy(wgr[:, :].rearrange("p (h d) -> p h d", d=DH),
                              wgr8[:, :].rearrange("p (h o) -> p h o", o=1).to_broadcast([64, 8, DH]))
                v.tensor_tensor(hrrows[:, :], hrrows[:, :], hrrows2[:, :], ALU.add)
                v.wait_ge(pe_ok, 5)
                for k, t in enumerate((src_i, dst_i, scat_i, dinv)):
                    v.tensor_copy(t[:, :].rearrange("p (j t) -> p j t", j=2),
                                  ps[0][:, 1024 + 256 * k:1024 + 256 * k + T].rearrange("p (j t) -> p j t", j=2))

        SUM, DIF, M2, NMEAN, VAR, EPS2, RSTD, NB = range(8)

        def row_stats(v, ch, st, sm, src, tiles, add_eps, signal):
            for w in range(tiles):
                ins = v.bn_stats(st[:, w, :], src[:, w, :])
            ch.link(ins)
            even, odd = st[:, 0:tiles, 1:3], st[:, 0:tiles, 4:6]
            t = slice(0, tiles)
            dif = ch.mark(v.tensor_tensor(sm[:, DIF, t], even[:, :, 0], odd[:, :, 0], ALU.subtract))
            total = ch.mark(v.tensor_tensor(sm[:, SUM, t], even[:, :, 0], odd[:, :, 0], ALU.add))
            ch.mark(v.scalar_tensor_tensor(out=sm[:, M2, t], in0=even[:, :, 1], scalar=C * EPS if add_eps else 0.0,
                                           in1=odd[:, :, 1], op0=ALU.add, op1=ALU.add))
            ch.wait(dif)
            square = ch.mark(v.scalar_tensor_tensor(out=sm[:, DIF, t], in0=sm[:, DIF, t], scalar=0.25,
                                                    in1=sm[:, DIF, t], op0=ALU.mult, op1=ALU.mult))
            ch.wait(total)
            v.tensor_scalar(sm[:, NMEAN, t], sm[:, SUM, t], -0.5, None, ALU.mult)
            ch.wait(square)
            ins = v.scalar_tensor_tensor(out=sm[:, VAR, t], in0=sm[:, M2, t], scalar=1.0 / C, in1=sm[:, DIF, t],
                                         op0=ALU.mult, op1=ALU.add)
            if not add_eps:
                ch.link(ins)
                ins = v.tensor_tensor(sm[:, VAR, t], sm[:, VAR, t], sm[:, EPS2, t], ALU.add)
            ins.then_inc(signal, 1)

        def relu_above_mean(v, ch, sm, dst, src, tiles):
            v.tensor_scalar(sm[:, EPS2, 0:tiles], sm[:, VAR, 0:tiles], EPS, None, ALU.mult)
            for w in range(tiles):
                ins = v.tensor_scalar(dst[:, w, :], src[:, w, :], sm[:, NMEAN, w:w + 1], 0.0, ALU.add, ALU.max)
            ch.link(ins)

        def inverse_root(g, link, at, sm, tiles, ready, signal, factor=None):
            t = slice(0, tiles)
            g.wait_ge(ready, at)
            g.tensor_tensor(sm[:, RSTD, t], sm[:, VAR, t], half[:, t], ALU.pow).then_inc(link, 1)
            steps = 1 if factor is None else 2
            if factor is not None:
                g.wait_ge(link, (at - 1) * steps + 1)
                g.tensor_tensor(sm[:, RSTD, t], sm[:, RSTD, t], factor, ALU.mult).then_inc(link, 1)
            g.wait_ge(link, (at - 1) * steps + steps)
            g.tensor_tensor(sm[:, NB, t], sm[:, NMEAN, t], sm[:, RSTD, t], ALU.mult).then_inc(signal, 1)

        def normalise(act, at, sm, dst, src, tiles, ready, signal):
            act.wait_ge(ready, at)
            for w in range(tiles):
                ins = act.activation(dst[:, w, :], src[:, w, :], ACT.Identity, scale=sm[:, RSTD, w:w + 1],
                                     bias=sm[:, NB, w:w + 1])
            ins.then_inc(signal, 1)

        def group_rows(t, g):
            width = t.shape[1]
            return t.rearrange("e c -> (e c)")[bass.ds(g * EG * width, EG * width)].rearrange(
                "(w p c) -> p w c", w=EW, p=P)

        def turns(h):
            return -(-(groups - h) // U)

        def mask_row(k, g):
            return masks[k][bass.ds(g * EG, EG)].rearrange("(o e) -> o e", o=1).to_broadcast([P, EG])

        def ebank(h, k):
            return bank(h // 2, 2 * (h % 2) + k)

        def etile(h, k, w, rows=P):
            return ps[h // 2][0:rows, 1024 * (h % 2) + 512 * k + w * C:1024 * (h % 2) + 512 * k + (w + 1) * C]

        def stage(eng, table, dst, at, staged):
            eng.tensor_copy(dst, table[:, bass.ds((at - 1) * EW, EW)]).then_inc(staged, 1)


        def gather(g, dst, table, index, signal, limit):
            for w in range(EW):
                g.indirect_dma_start(out=dst[:, w, :], out_offset=None, in_=table,
                                     in_offset=bass.IndirectOffsetOnAxis(ap=index[:, w:w + 1], axis=0),
                                     bounds_check=limit, oob_is_err=False).then_inc(signal, 16)

        def scatter(g, table, src, index, signal, limit):
            for w in range(EW):
                g.indirect_dma_start(out=table, out_offset=bass.IndirectOffsetOnAxis(ap=index[:, w:w + 1], axis=0),
                                     in_=src[:, w, :], in_offset=None,
                                     bounds_check=limit, oob_is_err=False).then_inc(signal, 16)

        def softmax_scans(v, ch, h, g, m, z, r, e, ab, neg, m_done):
            before = (h - 1) % U
            if not isinstance(g, int) or g:
                v.wait_ge(m_done, g)
                ch.link(v.tensor_copy(m[h][:, 0:1], m[before][:, EG:EG + 1]))
            else:
                ch.link(v.memset(m[h][:, 0:1], NEG))
            v.tensor_tensor_scan(m[h][:, 1:EG + 1], neg[h][:, :], e[h][:, :], m[h][:, 0:1], ALU.add, ALU.max
                                 ).then_inc(m_done, 1)
            v.wait_ge(m_done, g + 1)
            v.tensor_tensor(ab[h][:, 1, :], e[h][:, :], m[h][:, 1:EG + 1], ALU.subtract)
            ch.link(v.tensor_tensor(ab[h][:, 0, :], m[h][:, 0:EG], neg[h][:, :], ALU.add))

        def last_of(buf, h, g):
            return 0.0 if isinstance(g, int) and g == 0 else buf[(h - 1) % U][:, EG - 1:EG]


        with Phase(nc) as phase, ExitStack() as ctx:
            def sem(name):
                return phase.semaphore("node_" + name)

            def ring(name, depth):
                return [sb(f"node_{name}{k}", [P, W, C], F32, ctx) for k in range(depth)]

            x0, x2, x3 = ring("x0", 4), ring("x2", 4), ring("x3", 4)
            n0, hT0 = ring("n0", 2), ring("hT0", 1)
            u = ring("u", 4)
            n2 = ring("n2", 2)
            nh, hTh = ring("nh", 2), ring("hTh", 2)
            w = ring("w", 2)
            n3, hT3 = ring("n3", 2), ring("hT3", 1)

            NK = 4
            K0, K2, KH, K3 = range(NK)
            st = [[sb(f"st{k}_{h}", [P, W, 6], F32, ctx) for h in range(H)] for k in range(NK)]
            small = [[sb(f"small{k}_{h}", [P, 8, W], F32, ctx) for h in range(H)] for k in range(NK)]

            var_ready, rstd_ready, rows_ready, root_link, stats_link = (
                [sem(f"{n}{k}") for k in range(NK)]
                for n in ("var_ready", "rstd_ready", "rows_ready", "root_link", "stats_link"))
            last_ready = [sem(f"last_ready{k}") for k in range(NK)]
            mean_ready, passed = sem("mean_ready"), sem("passed")
            t0_ready, hT0_ready, mm0_ready = sem("t0_ready"), sem("hT0_ready"), sem("mm0_ready")
            th_ready, yT_ready, z_ready, y_ready = sem("th_ready"), sem("yT_ready"), sem("z_ready"), sem("y_ready")
            t3_ready, hT3_ready, mm3_ready = sem("t3_ready"), sem("hT3_ready"), sem("mm3_ready")
            x2_ready, gain_ready, h2_ready = sem("x2_ready"), sem("gain_ready"), sem("h2_ready")
            exp_ready, w_ready, yx_ready = sem("exp_ready"), sem("w_ready"), sem("yx_ready")
            x3_ready, out_ready = sem("x3_ready"), sem("out_ready")
            x_loaded, x2_stored, n2_stored, n3_stored, out_stored = (
                [sem(f"{n}{h}") for h in range(H)]
                for n in ("x_loaded", "x2_stored", "n2_stored", "n3_stored", "out_stored"))
            block = ctx.enter_context(nc.Block())

            AT = dict(LOAD=0.0, STATS0=0.296, ROOT0=0.43, NORM0=0.57, TURN0=0.986, RELU0=1.053, RES0=1.115,
                      X2=1.419, ST1=1.494, STATS2=1.606, ROOT2=1.981, NORM2=2.166, ST2=2.328, H2=2.559, STATSH=2.97,
                      ROOTH=3.109, NORMH=3.317, TURNH=3.479, YT=3.721, Z=3.793, Y=4.535, EXPZ=3.993, X3=4.782,
                      ELU=4.093, X3SUM=4.844, STATS3=5.156, ROOT3=5.29, NORM3=5.833, ST3=5.995, TURN3=6.042,
                      RELU3=6.109, OUT3=6.293, OUT=6.483, STO=6.567)

            bank0, bankh, banky, bank3 = (ps[k // 2][:, 1024 * (k % 2):1024 * (k % 2) + 1024] for k in range(4))

            def tile(pair, w):
                return pair[:, w * C:(w + 1) * C]

            def last(i, h):
                return isinstance(i, int) and i * H + h == nodes - 1

            def node_rows(t, i, h):
                start = N - GN if last(i, h) else (i * H + h) * GN
                return t.rearrange("n c -> (n c)")[bass.ds(start * C, GN * C)].rearrange("(p w) -> p w", p=P)

            def stored_at(stored, i, h, back):
                k = h - back
                return stored[k % H], 16 * (i + k // H + 1)

            def rows_free(eng, i, h, k):
                at = i * H + h + 1
                if k == K0:
                    wait(eng, t0_ready, at - 2)
                if k == K2:
                    wait(eng, *stored_at(n2_stored, i, h, 2))
                    wait(eng, gain_ready, at - 2)
                if k == KH:
                    wait(eng, th_ready, at - 2)
                if k == K3:
                    wait(eng, *stored_at(n3_stored, i, h, 2))
                    wait(eng, t3_ready, at - 2)

            def wait_rows(eng, k, value):
                wait(eng, rows_ready[k], value)
                wait(eng, last_ready[k], value)

            @block.sync
            def _(sp):
                def load(i, h):
                    wait(sp, x2_ready, (i - 1) * H + h + 1)
                    sp.dma_start(flat(x0[h]), node_rows(a["x"], i, h)).then_inc(x_loaded[h], 16)

                def store(i, h, table, src, ready, stored):
                    if ready in (K2, K3):
                        wait_rows(sp, ready, i * H + h + 1)
                    else:
                        sp.wait_ge(ready, i * H + h + 1)
                    if last(i, h):
                        sp.wait_ge(*stored_at(stored, i, h, 1))
                    sp.dma_start(node_rows(table, i, h), flat(src[h % len(src)])).then_inc(stored[h], 16)

                pipeline(sp, H, AT, nodes, {
                    "LOAD": load,
                    "ST1": lambda i, h: store(i, h, t_x1, x2, x2_ready, x2_stored),
                    "ST2": lambda i, h: store(i, h, t_n2, n2, K2, n2_stored),
                    "ST3": lambda i, h: store(i, h, t_n3, n3, K3, n3_stored),
                    "STO": lambda i, h: store(i, h, out, x3, out_ready, out_stored),
                })
                for h in range(H):
                    done = -(-(nodes - h) // H)
                    for stored in (x2_stored, n2_stored, n3_stored, out_stored):
                        sp.wait_ge(stored[h], 16 * done)

            @block.scalar
            def _(act):
                def normalise(i, h, k, dst, src):
                    act.wait_ge(rstd_ready[k], i * H + h + 1)
                    rows_free(act, i, h, k)
                    sm = small[k][h]
                    for t in range(W - 1):
                        ins = act.activation(dst[h % 2][:, t, :], src[h][:, t, :], ACT.Identity,
                                             scale=sm[:, RSTD, t:t + 1], bias=sm[:, NB, t:t + 1])
                    ins.then_inc(rows_ready[k], 1)

                def relu_t(i, h, dst, pair, ready, used, signal):
                    act.wait_ge(ready, i * H + h + 1)
                    wait(act, used, i * H + h)
                    act.activation(flat(dst[0]), pair, ACT.Relu).then_inc(signal, 1)

                def y_t(i, h):
                    act.wait_ge(th_ready, i * H + h + 1)
                    wait(act, z_ready, i * H + h - 1)
                    wait(act, y_ready, i * H + h - 1)
                    act.activation(flat(hTh[h % 2]), bankh, ACT.Identity, scale=col(G2), bias=col(S2)
                                   ).then_inc(yT_ready, 1)

                def exp_z(i, h):
                    act.wait_ge(z_ready, i * H + h + 1)
                    act.activation(flat(u[h]), bankh, ACT.Exp, bias=-1.0).then_inc(exp_ready, 1)

                def form_x3(i, h):
                    act.wait_ge(y_ready, i * H + h + 1)
                    wait(act, *stored_at(out_stored, i, h, 4))
                    act.activation(flat(x3[h]), banky, ACT.Identity, bias=-1.0).then_inc(yx_ready, 1)

                pipeline(act, H, AT, nodes, {
                    "NORM0": lambda i, h: normalise(i, h, K0, n0, x0),
                    "RELU0": lambda i, h: relu_t(i, h, hT0, bank0, t0_ready, mm0_ready, hT0_ready),
                    "NORM2": lambda i, h: normalise(i, h, K2, n2, u),
                    "NORMH": lambda i, h: normalise(i, h, KH, nh, u),
                    "YT": y_t,
                    "EXPZ": exp_z,
                    "X3": form_x3,
                    "NORM3": lambda i, h: normalise(i, h, K3, n3, x3),
                    "RELU3": lambda i, h: relu_t(i, h, hT3, bank3, t3_ready, mm3_ready, hT3_ready),
                })

            @block.gpsimd
            def _(g):
                def root(i, h, k, dst, src):
                    at, sm = i * H + h + 1, small[k][h]
                    inverse_root(g, root_link[k], at, sm, W, var_ready[k], rstd_ready[k])
                    g.wait_ge(rstd_ready[k], at)
                    rows_free(g, i, h, k)
                    g.sem_inc(passed, 1)
                    g.tensor_scalar(dst[h % 2][:, W - 1, :], src[h][:, W - 1, :], sm[:, RSTD, W - 1:W],
                                    sm[:, NB, W - 1:W], ALU.mult, ALU.add).then_inc(last_ready[k], 1)

                def wide(t):
                    return t[:, :].rearrange("p (o c) -> p o c", o=1).to_broadcast([P, W, C])

                def form_h2(i, h):
                    at = i * H + h + 1
                    wait_rows(g, K2, at)
                    g.tensor_tensor(u[h][:, :, :], n2[h % 2][:, :, :], wide(g1rows), ALU.mult).then_inc(gain_ready, 1)
                    g.wait_ge(gain_ready, at)
                    g.tensor_tensor(u[h][:, :, :], u[h][:, :, :], wide(hrrows), ALU.add).then_inc(h2_ready, 1)

                def add_w(i, h):
                    g.wait_ge(w_ready, i * H + h + 1)
                    g.wait_ge(yx_ready, i * H + h + 1)
                    g.tensor_tensor(x3[h][:, :, :], x3[h][:, :, :], w[h % 2][:, :, :], ALU.add).then_inc(x3_ready, 1)

                pipeline(g, H, AT, nodes, {
                    "ROOT0": lambda i, h: root(i, h, K0, n0, x0),
                    "ROOT2": lambda i, h: root(i, h, K2, n2, u),
                    "H2": form_h2,
                    "ROOTH": lambda i, h: root(i, h, KH, nh, u),
                    "X3SUM": add_w,
                    "ROOT3": lambda i, h: root(i, h, K3, n3, x3),
                })

            @block.tensor
            def _(pe):
                def transposes(i, h, pair, src, k, signal, free):
                    at = i * H + h + 1
                    wait_rows(pe, k, at)
                    wait(pe, free, at - 1)
                    for t in range(W):
                        ins = pe.transpose(tile(pair, t), src[h % 2][:, t, :], ident[:, :])
                    ins.then_inc(signal, 1)

                def product(i, h, pair, hT, ready, signal, weight, bias=None):
                    pe.wait_ge(ready, i * H + h + 1)
                    for t in range(W):
                        ins = pe.matmul(tile(pair, t), hT[h % len(hT)][:, t, :], weight[:, :], start=True,
                                        stop=bias is None)
                        if bias is not None:
                            ins = pe.matmul(tile(pair, t), ones3[:, :], bias[:, :], start=False, stop=True)
                    ins.then_inc(signal, 1)

                def y_rows(i, h):
                    at = i * H + h + 1
                    pe.wait_ge(yT_ready, at)
                    pe.wait_ge(x2_ready, at)
                    wait(pe, yx_ready, at - 1)
                    for t in range(W):
                        pe.matmul(tile(banky, t), hTh[h % 2][:, t, :], ident[:, :], start=True, stop=False)
                        ins = pe.matmul(tile(banky, t), ident[:, :], x2[h][:, t, :], start=False, stop=True)
                    ins.then_inc(y_ready, 1)

                pipeline(pe, H, AT, nodes, {
                    "TURN0": lambda i, h: transposes(i, h, bank0, n0, K0, t0_ready, x2_ready),
                    "RES0": lambda i, h: product(i, h, bank0, hT0, hT0_ready, mm0_ready, wres0, bias1),
                    "TURNH": lambda i, h: transposes(i, h, bankh, nh, KH, th_ready, w_ready),
                    "Z": lambda i, h: product(i, h, bankh, hTh, yT_ready, z_ready, wsi, biassi),
                    "Y": y_rows,
                    "TURN3": lambda i, h: transposes(i, h, bank3, n3, K3, t3_ready, out_ready),
                    "OUT3": lambda i, h: product(i, h, bank3, hT3, hT3_ready, mm3_ready, w3, bias3),
                })

            @block.vector
            def _(v):
                def stats(i, h, k, src, ready, value):
                    at = i * H + h + 1
                    v.wait_ge(ready, value)
                    wait_rows(v, k, at - H)
                    ch = Chain(v, stats_link[k], 5, at)
                    row_stats(v, ch, st[k][h], small[k][h], src[h], W, True, var_ready[k])
                    ch.end()

                def form_x2(i, h):
                    at = i * H + h + 1
                    v.wait_ge(mm0_ready, at)
                    wait(v, x2_stored[h], 16 * i)
                    wait(v, y_ready, at - H)
                    v.tensor_tensor(flat(x2[h]), bank0, flat(x0[h]), ALU.add).then_inc(x2_ready, 1)

                def stats2(i, h):
                    at = i * H + h + 1
                    v.wait_ge(x2_ready, at)
                    wait_rows(v, K2, at - H)
                    wait(v, w_ready, at - H)
                    ch = Chain(v, stats_link[K2], 12, at)
                    row_stats(v, ch, st[K2][h], small[K2][h], x2[h], W, True, mean_ready)
                    v.wait_ge(mean_ready, at)
                    relu_above_mean(v, ch, small[K2][h], u[h], x2[h], W)
                    row_stats(v, ch, st[K2][h], small[K2][h], u[h], W, False, var_ready[K2])
                    ch.end()

                def elu(i, h):
                    at = i * H + h + 1
                    v.wait_ge(exp_ready, at)
                    wait(v, x3_ready, at - 2)
                    v.scalar_tensor_tensor(out=flat(w[h % 2]), in0=flat(u[h]), scalar=1.0, in1=bankh,
                                           op0=ALU.min, op1=ALU.max).then_inc(w_ready, 1)

                def form_out(i, h):
                    at = i * H + h + 1
                    v.wait_ge(mm3_ready, at)
                    wait_rows(v, K3, at)
                    v.scalar_tensor_tensor(out=flat(x3[h]), in0=bank3, scalar=0.0, in1=flat(x3[h]),
                                           op0=ALU.max, op1=ALU.add).then_inc(out_ready, 1)

                pipeline(v, H, AT, nodes, {
                    "STATS0": lambda i, h: stats(i, h, K0, x0, x_loaded[h], 16 * (i + 1)),
                    "X2": form_x2,
                    "STATS2": stats2,
                    "STATSH": lambda i, h: stats(i, h, KH, u, h2_ready, i * H + h + 1),
                    "ELU": elu,
                    "STATS3": lambda i, h: stats(i, h, K3, x3, x3_ready, i * H + h + 1),
                    "OUT": form_out,
                })
        with Phase(nc) as phase, ExitStack() as ctx:
            def sem(name):
                return phase.semaphore("l0_" + name)

            def bufs(name, shape, dt=F32):
                return [sb(f"l0_{name}{h}", shape, dt, ctx) for h in range(U)]

            def sems(name):
                return [sem(f"{name}{h}") for h in range(U)]

            xin = bufs("xin", [P, 2 * EW, C])
            nrm = bufs("nrm", [P, 2 * EW, C])
            hT = bufs("hT", [P, 2, EG])
            q = bufs("q", [P, EG])
            kq = bufs("kq", [P, EG])
            e = bufs("e", [P, EG])
            neg = bufs("neg", [P, EG])
            m = bufs("m", [P, EG + 1])
            z = bufs("z", [P, EG])
            rs = bufs("rs", [P, EG])
            r = bufs("r", [P, EG])
            ab = bufs("ab", [P, 2, EG])
            xo = bufs("xo", [P, EW, C])
            st = bufs("st", [P, 2 * EW, 6])
            small = bufs("small", [P, 8, 2 * EW])
            index = bufs("index", [P, 3, EW], I32)
            gathered, stored, scattered, neg_in = sems("gathered"), sems("stored"), sems("scattered"), sems("neg_in")
            stats_link, max_link, sum_link = sem("stats_link"), sem("max_link"), sem("sum_link")
            (staged, passed, var_ready, root_link, rstd_ready, rows_ready, t_ready, hT_ready, kq_ready, q_ready,
             prod_ready, ev_ready, e_ready, m_done, ab_ready, exp_ready, z_done, r_done, rst_ready, sum_ready,
             x1_ready, scat_staged) = [sem(n) for n in (
                 "staged", "passed", "var_ready", "root_link", "rstd_ready", "rows_ready", "t_ready", "hT_ready",
                 "kq_ready", "q_ready", "prod_ready", "ev_ready", "e_ready", "m_done", "ab_ready", "exp_ready",
                 "z_done", "r_done", "rst_ready", "sum_ready", "x1_ready", "scat_staged")]
            block = ctx.enter_context(nc.Block())
            AT = dict(INDEX=0.0, GATHER=0.500, GATHER2=1.211, LOADM=0.500, STATS=1.942, ROOT=2.085, NORM=2.272,
                      TURN=2.487, RELU=2.742, KQ=2.814, Q=2.945, PROD=3.072, EV=3.125, ESC=3.474, MAXI=3.519,
                      EXPO=3.801, SUMS=4.112, RES=4.566, X1=4.747, ST=4.996, PUT=4.799)

            @block.sync
            def _(sp):
                def load(i, h):
                    wait(sp, ab_ready, (i - 1) * U + h + 1)
                    sp.dma_start(neg[h][:, :], mask_row(1, i * U + h)).then_inc(neg_in[h], 16)

                def store(i, h):
                    sp.wait_ge(x1_ready, i * U + h + 1)
                    sp.dma_start(group_rows(x1_e, i * U + h), xo[h][:, :, :]).then_inc(stored[h], 16)

                pipeline(sp, U, AT, groups, {"LOADM": load, "ST": store})
                for h in range(U):
                    sp.wait_ge(stored[h], 16 * turns(h))

            @block.gpsimd
            def _(g):
                limit = g.to_reg(N - 1)

                def fetch(i, h):
                    at = i * U + h + 1
                    wait(g, rows_ready, at - U)
                    g.wait_ge(staged, at)
                    g.sem_inc(passed, 1)
                    gather(g, xin[h][:, 0:EW, :], a["x"], index[h][:, 0, :], gathered[h], limit)

                def fetch_ends(i, h):
                    at = i * U + h + 1
                    wait(g, x1_ready, at - U)
                    g.wait_ge(staged, at)
                    g.sem_inc(passed, 1)
                    gather(g, xin[h][:, EW:2 * EW, :], a["x"], index[h][:, 1, :], gathered[h], limit)

                def put(i, h):
                    at = i * U + h + 1
                    g.wait_ge(x1_ready, at)
                    g.wait_ge(scat_staged, at)
                    g.sem_inc(passed, 1)
                    scatter(g, t_x1, xo[h], index[h][:, 2, :], scattered[h], limit)

                pipeline(g, U, AT, groups, {
                    "GATHER": fetch,
                    "GATHER2": fetch_ends,
                    "ROOT": lambda i, h: inverse_root(g, root_link, i * U + h + 1, small[h], 2 * EW, var_ready,
                                                    rstd_ready),
                    "PUT": put,
                })
                for h in range(U):
                    g.wait_ge(scattered[h], 16 * EW * turns(h))

            @block.scalar
            def _(act):
                def norm(i, h):
                    at = i * U + h + 1
                    wait(act, t_ready, at - U)
                    normalise(act, at, small[h], nrm[h], xin[h], 2 * EW, rstd_ready, rows_ready)

                def relu_t(i, h):
                    at = i * U + h + 1
                    act.wait_ge(t_ready, at)
                    wait(act, sum_ready, at - U)
                    act.activation(hT[h][:, :, :], ps[h // 2][:, 1024 * (h % 2):1024 * (h % 2) + 1024].rearrange(
                        "p (k c) -> p k c", k=2), ACT.Relu).then_inc(hT_ready, 1)

                def copy_q(i, h):
                    at = i * U + h + 1
                    act.wait_ge(kq_ready, at)
                    wait(act, prod_ready, at - U)
                    act.activation(q[h][:, :], ebank(h, 1), ACT.Identity).then_inc(q_ready, 1)

                def copy_e(i, h):
                    at = i * U + h + 1
                    act.wait_ge(ev_ready, at)
                    wait(act, rst_ready, at - U)
                    act.activation(e[h][:, :], ebank(h, 1), ACT.Identity).then_inc(e_ready, 1)

                def exps(i, h):
                    act.wait_ge(ab_ready, i * U + h + 1)
                    act.activation(ab[h][:, :, :], ab[h][:, :, :], ACT.Exp).then_inc(exp_ready, 1)

                pipeline(act, U, AT, groups, {"NORM": norm, "RELU": relu_t, "Q": copy_q, "ESC": copy_e, "EXPO": exps})

            @block.tensor
            def _(pe):
                def turn_rows(i, h):
                    at = i * U + h + 1
                    pe.wait_ge(rows_ready, at)
                    wait(pe, x1_ready, at - U)
                    for w in range(2 * EW):
                        ins = pe.transpose(etile(h, w // EW, w % EW), nrm[h][:, w, :], ident[:, :])
                    ins.then_inc(t_ready, 1)

                def k_and_q(i, h):
                    pe.wait_ge(hT_ready, i * U + h + 1)
                    pe.matmul(ebank(h, 0), wqkv[:, 1, :], hT[h][:, 0, :], start=True, stop=True)
                    pe.matmul(ebank(h, 1), wqkv[:, 0, :], hT[h][:, 1, :], start=True, stop=True).then_inc(kq_ready, 1)

                def e_and_v(i, h):
                    at = i * U + h + 1
                    pe.wait_ge(prod_ready, at)
                    pe.matmul(ebank(h, 1), heads[:, :], kq[h][:, :], start=True, stop=True)
                    pe.matmul(ebank(h, 0), wqkv[:, 2, :], hT[h][:, 0, :], start=True, stop=True).then_inc(ev_ready, 1)

                def sums(i, h):
                    at = i * U + h + 1
                    pe.wait_ge(rst_ready, at)
                    for w in range(EW):
                        t = slice(w * C, (w + 1) * C)
                        pe.matmul(etile(h, 1, w), hT[h][:, 1, t], wres0[:, :], start=True, stop=False)
                        pe.matmul(etile(h, 1, w), r[h][:, t], ident[:, :], start=False, stop=False)
                        ins = pe.matmul(etile(h, 1, w), ones3[:, :], bias1[:, :], start=False, stop=True)
                    ins.then_inc(sum_ready, 1)

                pipeline(pe, U, AT, groups, {"TURN": turn_rows, "KQ": k_and_q, "EV": e_and_v, "RES": sums})

            @block.vector
            def _(v):
                def stats(i, h):
                    ch = Chain(v, stats_link, 5, i * U + h + 1)
                    v.wait_ge(gathered[h], 16 * 2 * EW * (i + 1))
                    wait(v, rows_ready, (i - 1) * U + h + 1)
                    row_stats(v, ch, st[h], small[h], xin[h], 2 * EW, True, var_ready)
                    ch.end()

                def indices(i, h):
                    at = i * U + h + 1
                    wait(v, gathered[h], 16 * 2 * EW * i)
                    v.tensor_copy(index[h][:, 0, :], src_i[:, bass.ds((at - 1) * EW, EW)])
                    stage(v, dst_i, index[h][:, 1, :], at, staged)

                def product(i, h):
                    at = i * U + h + 1
                    v.wait_ge(q_ready, at)
                    v.tensor_tensor(kq[h][:, :], ebank(h, 0), q[h][:, :], ALU.mult).then_inc(prod_ready, 1)

                def maxima(i, h):
                    at = i * U + h + 1
                    ch = Chain(v, max_link, 3, at)
                    v.wait_ge(e_ready, at)
                    v.wait_ge(neg_in[h], 16 * (i + 1))
                    ch.link(v.scalar_tensor_tensor(out=e[h][:, :], in0=e[h][:, :], scalar=SLOPE, in1=e[h][:, :],
                                                      op0=ALU.mult, op1=ALU.max))
                    softmax_scans(v, ch, h, i * U + h, m, z, r, e, ab, neg, m_done)
                    v.tensor_tensor(ab[h][:, 0, :], ab[h][:, 0, :], m[h][:, 1:EG + 1], ALU.subtract
                                    ).then_inc(ab_ready, 1)

                def weighted(i, h):
                    at = i * U + h + 1
                    g = i * U + h
                    ch = Chain(v, sum_link, 2, at)
                    v.wait_ge(exp_ready, at)
                    wait(v, z_done, g)
                    v.tensor_tensor_scan(z[h][:, :], ab[h][:, 0, :], ab[h][:, 1, :], last_of(z, h, g), ALU.mult,
                                         ALU.add).then_inc(z_done, 1)
                    v.wait_ge(ev_ready, at)
                    ch.link(v.tensor_tensor(ab[h][:, 1, :], ebank(h, 0), ab[h][:, 1, :], ALU.mult))
                    wait(v, r_done, g)
                    wait(v, sum_ready, at - U)
                    v.tensor_tensor_scan(rs[h][:, :], ab[h][:, 0, :], ab[h][:, 1, :], last_of(rs, h, g), ALU.mult,
                                         ALU.add).then_inc(r_done, 1)
                    v.wait_ge(z_done, at)
                    ch.link(v.reciprocal(e[h][:, :], z[h][:, :]))
                    v.wait_ge(r_done, at)
                    v.tensor_tensor(r[h][:, :], rs[h][:, :], e[h][:, :], ALU.mult).then_inc(rst_ready, 1)

                def form_x1(i, h):
                    at = i * U + h + 1
                    v.wait_ge(sum_ready, at)
                    wait(v, stored[h], 16 * i)
                    wait(v, scattered[h], 16 * EW * i)
                    stage(v, scat_i, index[h][:, 2, :], at, scat_staged)
                    v.tensor_tensor(flat(xo[h]), ebank(h, 1), flat(xin[h][:, EW:2 * EW, :]), ALU.add
                                    ).then_inc(x1_ready, 1)


                pipeline(v, U, AT, groups, {"INDEX": indices, "STATS": stats,
                                            "PROD": product, "MAXI": maxima, "SUMS": weighted,
                                               "X1": form_x1})

        with Phase(nc) as phase, ExitStack() as ctx:
            def sem(name):
                return phase.semaphore("l1_" + name)

            def bufs(name, shape, dt=F32):
                return [sb(f"l1_{name}{h}", shape, dt, ctx) for h in range(U)]

            def sems(name):
                return [sem(f"{name}{h}") for h in range(U)]

            xin = bufs("xin", [P, EW, C])
            xe = bufs("xe", [P, EW, C])
            nrm = bufs("nrm", [P, EW, C])
            hT = bufs("hT", [P, EG])
            attr = bufs("attr", [P, EW, 16])
            attrT = bufs("attrT", [16, EG])
            ew = bufs("ew", [P, EG])
            msg = bufs("msg", [P, EG])
            agg = bufs("agg", [P, EG])
            same = bufs("same", [P, EG])
            x2 = bufs("x2", [P, EW, C])
            u = bufs("u", [P, EW, C])
            n2 = bufs("n2", [P, EW, C])
            st = bufs("st", [P, EW, 6])
            small = bufs("small", [P, 8, EW])
            index = bufs("index", [P, 2, EW], I32)
            gathered, stored, scattered, loaded = (sems(n) for n in ("gathered", "stored", "scattered", "loaded"))
            stats_link, agg_link, stats2_link = sem("stats_link"), sem("agg_link"), sem("stats2_link")
            (staged, passed, var_ready, root_link, rstd_ready, rows_ready, t_ready, hT_ready, prod_ready, ew_ready,
             agg_done, back_ready, x2_ready, var2a, var2_ready, root2_link, rstd2_ready, n2_ready,
             scat_staged) = [sem(n) for n in (
                 "staged", "passed", "var_ready", "root_link", "rstd_ready", "rows_ready", "t_ready", "hT_ready",
                 "prod_ready", "ew_ready", "agg_done", "back_ready", "x2_ready", "var2a", "var2_ready",
                 "root2_link", "rstd2_ready", "n2_ready", "scat_staged")]
            block = ctx.enter_context(nc.Block())
            AT = dict(INDEX=0.0, GATHER=0.500, LOAD=0.500, STATS=1.450, ROOT=1.892, NORM=2.013, TURN=2.171,
                      RELU=2.373, XW=2.490, EWC=2.662, AGG=2.723, BACK=2.858, X2=2.930, ST=3.002, NORMS2=3.055,
                      ROOT2=3.388, N2=3.510, PUT=3.995)

            @block.sync
            def _(sp):
                def load(i, h):
                    g = i * U + h
                    wait(sp, x2_ready, g + 1 - U)
                    sp.dma_start(xe[h][:, :, :], group_rows(x1_e, g)).then_inc(loaded[h], 16)
                    sp.dma_start(attr[h][:, :, :], group_rows(attr_e, g)).then_inc(loaded[h], 16)
                    sp.dma_start(same[h][:, :], mask_row(0, g)).then_inc(loaded[h], 16)

                def store(i, h):
                    sp.wait_ge(x2_ready, i * U + h + 1)
                    sp.dma_start(group_rows(x2_e, i * U + h), x2[h][:, :, :]).then_inc(stored[h], 16)

                pipeline(sp, U, AT, groups, {"LOAD": load, "ST": store})
                for h in range(U):
                    sp.wait_ge(stored[h], 16 * turns(h))

            @block.gpsimd
            def _(g):
                limit = g.to_reg(N - 1)

                def fetch(i, h):
                    at = i * U + h + 1
                    wait(g, rows_ready, at - U)
                    g.wait_ge(staged, at)
                    g.sem_inc(passed, 1)
                    gather(g, xin[h], t_x1, index[h][:, 0, :], gathered[h], limit)

                def put(i, h):
                    at = i * U + h + 1
                    g.wait_ge(n2_ready, at)
                    g.wait_ge(scat_staged, at)
                    g.sem_inc(passed, 1)
                    scatter(g, t_n2, n2[h], index[h][:, 1, :], scattered[h], limit)

                pipeline(g, U, AT, groups, {
                    "GATHER": fetch,
                    "ROOT": lambda i, h: inverse_root(g, root_link, i * U + h + 1, small[h], EW, var_ready, rstd_ready),
                    "ROOT2": lambda i, h: inverse_root(g, root2_link, i * U + h + 1, small[h], EW, var2_ready,
                                                     rstd2_ready),
                    "PUT": put,
                })
                for h in range(U):
                    g.wait_ge(scattered[h], 16 * EW * turns(h))

            @block.scalar
            def _(act):
                def norm(i, h):
                    at = i * U + h + 1
                    wait(act, t_ready, at - U)
                    normalise(act, at, small[h], nrm[h], xin[h], EW, rstd_ready, rows_ready)

                def relu_t(i, h):
                    at = i * U + h + 1
                    act.wait_ge(t_ready, at)
                    wait(act, prod_ready, at - U)
                    act.activation(hT[h][:, :], ebank(h, 0), ACT.Relu)
                    act.activation(attrT[h][:, :], ebank(h, 1)[0:16, :], ACT.Identity).then_inc(hT_ready, 1)

                def copy_ew(i, h):
                    at = i * U + h + 1
                    act.wait_ge(prod_ready, at)
                    wait(act, agg_done, at - U)
                    act.activation(ew[h][:, :], ebank(h, 1), ACT.Identity).then_inc(ew_ready, 1)

                def norm2(i, h):
                    at = i * U + h + 1
                    wait(act, scattered[h], 16 * EW * i)
                    normalise(act, at, small[h], n2[h], u[h], EW, rstd2_ready, n2_ready)

                pipeline(act, U, AT, groups, {"NORM": norm, "RELU": relu_t, "EWC": copy_ew, "N2": norm2})

            @block.tensor
            def _(pe):
                def turn_rows(i, h):
                    at = i * U + h + 1
                    pe.wait_ge(rows_ready, at)
                    pe.wait_ge(loaded[h], 48 * (i + 1))
                    wait(pe, x2_ready, at - U)
                    for w in range(EW):
                        pe.transpose(etile(h, 0, w), nrm[h][:, w, :], ident[:, :])
                        ins = pe.transpose(etile(h, 1, w, 16), attr[h][:, w, :], ident[:, :])
                    ins.then_inc(t_ready, 1)

                def products(i, h):
                    pe.wait_ge(hT_ready, i * U + h + 1)
                    pe.matmul(ebank(h, 0), w1[:, :], hT[h][:, :], start=True, stop=True)
                    pe.matmul(ebank(h, 1), edge_w[:, :], attrT[h][:, :], start=True, stop=True).then_inc(prod_ready, 1)

                def back(i, h):
                    pe.wait_ge(agg_done, i * U + h + 1)
                    for w in range(EW):
                        ins = pe.transpose(etile(h, 0, w), agg[h][:, w * C:(w + 1) * C], ident[:, :])
                    ins.then_inc(back_ready, 1)

                pipeline(pe, U, AT, groups, {"TURN": turn_rows, "XW": products, "BACK": back})

            @block.vector
            def _(v):
                def stats(i, h):
                    ch = Chain(v, stats_link, 6, i * U + h + 1)
                    v.wait_ge(gathered[h], 16 * EW * (i + 1))
                    wait(v, n2_ready, (i - 1) * U + h + 1)
                    ch.link(v.tensor_tensor(xin[h][:, :, :], xin[h][:, :, :],
                                            b1rows[:, :].rearrange("p (o c) -> p o c", o=1).to_broadcast([P, EW, C]),
                                            ALU.subtract))
                    row_stats(v, ch, st[h], small[h], xin[h], EW, True, var_ready)
                    ch.end()

                def indices(i, h):
                    wait(v, gathered[h], 16 * EW * i)
                    stage(v, src_i, index[h][:, 0, :], i * U + h + 1, staged)

                def aggregate(i, h):
                    at, g = i * U + h + 1, i * U + h
                    ch = Chain(v, agg_link, 1, at)
                    v.wait_ge(ew_ready, at)
                    ch.link(v.tensor_tensor(msg[h][:, :], ebank(h, 0), ew[h][:, :], ALU.mult))
                    v.wait_ge(loaded[h], 48 * (i + 1))
                    wait(v, agg_done, g)
                    wait(v, back_ready, at - U)
                    v.tensor_tensor_scan(agg[h][:, :], same[h][:, :], msg[h][:, :], last_of(agg, h, g), ALU.mult,
                                         ALU.add).then_inc(agg_done, 1)

                def form_x2(i, h):
                    at = i * U + h + 1
                    v.wait_ge(back_ready, at)
                    v.wait_ge(loaded[h], 48 * (i + 1))
                    wait(v, stored[h], 16 * i)
                    v.tensor_tensor(flat(x2[h]), ebank(h, 0), flat(xe[h]), ALU.add).then_inc(x2_ready, 1)

                def norms2(i, h):
                    at = i * U + h + 1
                    ch = Chain(v, stats2_link, 12, at)
                    v.wait_ge(x2_ready, at)
                    v.wait_ge(rows_ready, at)
                    wait(v, scattered[h], 16 * EW * i)
                    stage(v, scat_i, index[h][:, 1, :], at, scat_staged)
                    row_stats(v, ch, st[h], small[h], x2[h], EW, True, var2a)
                    v.wait_ge(var2a, at)
                    relu_above_mean(v, ch, small[h], u[h], x2[h], EW)
                    row_stats(v, ch, st[h], small[h], u[h], EW, False, var2_ready)
                    ch.end()

                pipeline(v, U, AT, groups, {"INDEX": indices, "STATS": stats, "AGG": aggregate,
                                            "X2": form_x2, "NORMS2": norms2})

        with Phase(nc) as phase, ExitStack() as ctx:
            def sem(name):
                return phase.semaphore("l2_" + name)

            def bufs(name, shape, dt=F32):
                return [sb(f"l2_{name}{h}", shape, dt, ctx) for h in range(U)]

            def sems(name):
                return [sem(f"{name}{h}") for h in range(U)]

            xin = bufs("xin", [P, 2 * EW, C])
            hT = bufs("hT", [P, 2, EG])
            fs = bufs("fs", [P, EG])
            fd = bufs("fd", [P, EG])
            e = bufs("e", [P, EG])
            pool = bufs("pool", [P, EG])
            pm = bufs("pm", [P, EG])
            neg = bufs("neg", [P, EG])
            m = bufs("m", [P, EG + 1])
            z = bufs("z", [P, EG])
            r = bufs("r", [P, EG])
            ab = bufs("ab", [P, 2, EG])
            gf = bufs("gf", [64, EG])
            xe = bufs("xe", [P, EW, C])
            h2 = bufs("h2", [P, EW, C])
            x3 = bufs("x3", [P, EW, C])
            n3 = bufs("n3", [P, EW, C])
            st = bufs("st", [P, EW, 6])
            small = bufs("small", [P, 8, EW])
            index = bufs("index", [P, 3, EW], I32)
            gathered, stored, scattered, loaded = (sems(n) for n in ("gathered", "stored", "scattered", "loaded"))
            max_link, sum_link, att_link, statsh_link, stats3_link = [sem(n) for n in (
                "max_link", "sum_link", "att_link", "statsh_link", "stats3_link")]
            (staged, passed, t_ready, hT_ready, f_ready, fc_ready, prod_ready, ep_ready, e_ready, m_done, pm_done,
             ab_ready, exp_ready, z_done, r_done, agg_ready, gf_ready, gfc_ready, gate_ready, ex_ready, att_ready,
             h2_sum, h2_ready, varh_ready, rooth_link, rstdh_ready, nh_ready, th_ready, yT_ready, y_ready, y_used,
             zz_ready, ez_ready, w_done, x3_ready, var3_ready, root3_link, rstd3_ready, n3_ready, scat_staged) = [
                 sem(n) for n in (
                     "staged", "passed", "t_ready", "hT_ready", "f_ready", "fc_ready", "prod_ready", "ep_ready",
                     "e_ready", "m_done", "pm_done", "ab_ready", "exp_ready", "z_done", "r_done", "agg_ready",
                     "gf_ready", "gfc_ready", "gate_ready", "ex_ready", "att_ready", "h2_sum", "h2_ready",
                     "varh_ready", "rooth_link", "rstdh_ready", "nh_ready", "th_ready", "yT_ready", "y_ready",
                     "y_used", "zz_ready", "ez_ready", "w_done", "x3_ready", "var3_ready", "root3_link",
                     "rstd3_ready", "n3_ready", "scat_staged")]
            block = ctx.enter_context(nc.Block())
            AT = dict(GATHER=0.0, GATHER2=0.631, LOAD=0.0, TURN=1.261, GAIN=1.345, FEAT=1.422, FC=1.536, PROD=1.606,
                      EP=1.669, EC=1.783, MAXI=1.858, EXPO=2.085, GF=2.085, GFC=2.206, GATE=2.333, SUMS=2.153,
                      EX=2.632, ATT=2.704, HSUM=2.829, HC=2.961, STATSH=3.073, ROOTH=3.26, NH=3.41, TH=3.545,
                      YT=3.594, Y=3.771, ZZ=3.949, X3=3.819, EZ=4.141, ELU=4.518, ST1=4.614, STATS3=4.63,
                      ROOT3=4.891, N3=4.989, ST2=5.094, PUT=5.332)

            @block.sync
            def _(sp):
                def load(i, h):
                    g = i * U + h
                    wait(sp, x3_ready, g + 1 - U)
                    sp.dma_start(xe[h][:, :, :], group_rows(x2_e, g)).then_inc(loaded[h], 16)
                    sp.dma_start(neg[h][:, :], mask_row(1, g)).then_inc(loaded[h], 16)

                def store_x3(i, h):
                    sp.wait_ge(x3_ready, i * U + h + 1)
                    sp.dma_start(group_rows(x3_e, i * U + h), x3[h][:, :, :]).then_inc(stored[h], 16)

                def store_n3(i, h):
                    sp.wait_ge(n3_ready, i * U + h + 1)
                    sp.dma_start(group_rows(n3_e, i * U + h), n3[h][:, :, :]).then_inc(stored[h], 16)

                pipeline(sp, U, AT, groups, {"LOAD": load, "ST1": store_x3, "ST2": store_n3})
                for h in range(U):
                    sp.wait_ge(stored[h], 32 * turns(h))

            @block.gpsimd
            def _(g):
                limit = g.to_reg(N - 1)

                def fetch(i, h):
                    at = i * U + h + 1
                    wait(g, t_ready, at - U)
                    g.sem_inc(passed, 1)
                    stage(g, src_i, index[h][:, 0, :], at, staged)
                    g.tensor_copy(index[h][:, 1, :], dst_i[:, bass.ds((at - 1) * EW, EW)]).then_inc(staged, 1)
                    g.wait_ge(staged, 2 * at)
                    g.sem_inc(passed, 1)
                    gather(g, xin[h][:, 0:EW, :], t_n2, index[h][:, 0, :], gathered[h], limit)

                def fetch_ends(i, h):
                    gather(g, xin[h][:, EW:2 * EW, :], t_n2, index[h][:, 1, :], gathered[h], limit)

                def put(i, h):
                    at = i * U + h + 1
                    g.wait_ge(n3_ready, at)
                    g.sem_inc(passed, 1)
                    stage(g, scat_i, index[h][:, 2, :], at, scat_staged)
                    g.wait_ge(scat_staged, at)
                    g.sem_inc(passed, 1)
                    scatter(g, t_n3, n3[h], index[h][:, 2, :], scattered[h], limit)

                pipeline(g, U, AT, groups, {
                    "GATHER": fetch,
                    "GATHER2": fetch_ends,
                    "ROOTH": lambda i, h: inverse_root(g, rooth_link, i * U + h + 1, small[h], EW, varh_ready,
                                                     rstdh_ready),
                    "ROOT3": lambda i, h: inverse_root(g, root3_link, i * U + h + 1, small[h], EW, var3_ready,
                                                     rstd3_ready, dinv[:, bass.ds((i * U + h) * EW, EW)]),
                    "PUT": put,
                })
                for h in range(U):
                    g.wait_ge(scattered[h], 16 * EW * turns(h))

            @block.scalar
            def _(act):
                def gain(i, h):
                    at = i * U + h + 1
                    act.wait_ge(t_ready, at)
                    wait(act, h2_sum, at - U)
                    act.activation(hT[h][:, :, :], ps[h // 2][:, 1024 * (h % 2):1024 * (h % 2) + 1024].rearrange(
                        "p (k c) -> p k c", k=2), ACT.Identity, scale=col(G1), bias=col(S1)).then_inc(hT_ready, 1)

                def copy_f(i, h):
                    at = i * U + h + 1
                    act.wait_ge(f_ready, at)
                    wait(act, h2_sum, at - U)
                    act.activation(fs[h][:, :], ebank(h, 0), ACT.Identity)
                    act.activation(fd[h][:, :], ebank(h, 1), ACT.Identity).then_inc(fc_ready, 1)

                def copy_e(i, h):
                    at = i * U + h + 1
                    act.wait_ge(ep_ready, at)
                    wait(act, att_ready, at - U)
                    act.activation(e[h][:, :], ebank(h, 0), ACT.Identity, scale=1.0 / DH ** 0.5)
                    act.activation(pool[h][:, :], ebank(h, 1), ACT.Relu, bias=col(BPOOL)).then_inc(e_ready, 1)

                def exps(i, h):
                    act.wait_ge(ab_ready, i * U + h + 1)
                    act.activation(ab[h][:, :, :], ab[h][:, :, :], ACT.Exp).then_inc(exp_ready, 1)

                def gate_bias(i, h):
                    at = i * U + h + 1
                    act.wait_ge(gf_ready, at)
                    wait(act, gate_ready, at - U)
                    act.activation(gf[h][:, :], ebank(h, 0)[0:64, :], ACT.Identity, bias=bgate[:, :]
                                   ).then_inc(gfc_ready, 1)

                def gate_exp(i, h):
                    at = i * U + h + 1
                    act.wait_ge(gate_ready, at)
                    act.wait_ge(agg_ready, at)
                    act.activation(ab[h][:, 0, :], ebank(h, 1), ACT.Tanh, scale=0.5, bias=col(HBGR))
                    act.activation(ab[h][:, 1, :], fd[h][:, :], ACT.Exp).then_inc(ex_ready, 1)

                def copy_h2(i, h):
                    at = i * U + h + 1
                    act.wait_ge(h2_sum, at)
                    wait(act, w_done, at - U)
                    act.activation(flat(h2[h]), ebank(h, 0), ACT.Identity).then_inc(h2_ready, 1)

                def norm_h(i, h):
                    at = i * U + h + 1
                    wait(act, stored[h], 32 * i)
                    wait(act, scattered[h], 16 * EW * i)
                    normalise(act, at, small[h], n3[h], h2[h], EW, rstdh_ready, nh_ready)

                def y_t(i, h):
                    at = i * U + h + 1
                    act.wait_ge(th_ready, at)
                    act.activation(pool[h][:, :], ebank(h, 0), ACT.Identity, scale=col(G2), bias=col(S2)
                                   ).then_inc(yT_ready, 1)

                def exp_z(i, h):
                    act.wait_ge(zz_ready, i * U + h + 1)
                    act.activation(flat(h2[h]), ebank(h, 0), ACT.Exp, bias=-1.0).then_inc(ez_ready, 1)

                def norm3(i, h):
                    at = i * U + h + 1
                    act.wait_ge(th_ready, at)
                    normalise(act, at, small[h], n3[h], x3[h], EW, rstd3_ready, n3_ready)

                pipeline(act, U, AT, groups, {"GAIN": gain, "FC": copy_f, "EC": copy_e, "EXPO": exps, "GFC": gate_bias,
                                                 "EX": gate_exp, "HC": copy_h2, "NH": norm_h, "YT": y_t, "EZ": exp_z,
                                                 "N3": norm3})

            @block.tensor
            def _(pe):
                def turn_rows(i, h):
                    at = i * U + h + 1
                    pe.wait_ge(gathered[h], 16 * 2 * EW * (i + 1))
                    wait(pe, w_done, at - U)
                    for w in range(2 * EW):
                        ins = pe.transpose(etile(h, w // EW, w % EW), xin[h][:, w, :], ident[:, :])
                    ins.then_inc(t_ready, 1)

                def features(i, h):
                    pe.wait_ge(hT_ready, i * U + h + 1)
                    pe.matmul(ebank(h, 0), wattn[:, :], hT[h][:, 0, :], start=True, stop=True)
                    pe.matmul(ebank(h, 1), wattn[:, :], hT[h][:, 1, :], start=True, stop=True).then_inc(f_ready, 1)

                def e_and_pool(i, h):
                    pe.wait_ge(prod_ready, i * U + h + 1)
                    pe.matmul(ebank(h, 0), heads[:, :], e[h][:, :], start=True, stop=True)
                    pe.matmul(ebank(h, 1), wpool[:, :], hT[h][:, 0, :], start=True, stop=True).then_inc(ep_ready, 1)

                def gate_features(i, h):
                    at = i * U + h + 1
                    pe.wait_ge(pm_done, at)
                    pe.wait_ge(e_ready, at)
                    pe.matmul(ebank(h, 0)[0:64, :], wgself[:, :], hT[h][:, 1, :], start=True, stop=False)
                    pe.matmul(ebank(h, 0)[0:64, :], wgneigh[:, :], pm[h][:, :], start=False, stop=True
                              ).then_inc(gf_ready, 1)

                def gate(i, h):
                    pe.wait_ge(gfc_ready, i * U + h + 1)
                    pe.matmul(ebank(h, 1), wgr[:, :], gf[h][:, :], start=True, stop=True).then_inc(gate_ready, 1)

                def h2_rows(i, h):
                    pe.wait_ge(att_ready, i * U + h + 1)
                    for w in range(EW):
                        t = slice(w * C, (w + 1) * C)
                        pe.matmul(etile(h, 0, w), fd[h][:, t], whr[:, :], start=True, stop=False)
                        pe.matmul(etile(h, 0, w), hT[h][:, 1, t], ident[:, :], start=False, stop=False)
                        ins = pe.matmul(etile(h, 0, w), ones3[:, :], biashr[:, :], start=False, stop=True)
                    ins.then_inc(h2_sum, 1)

                def turn_h(i, h):
                    at = i * U + h + 1
                    pe.wait_ge(nh_ready, at)
                    for w in range(EW):
                        ins = pe.transpose(etile(h, 0, w), n3[h][:, w, :], ident[:, :])
                    ins.then_inc(th_ready, 1)

                def y_rows(i, h):
                    pe.wait_ge(yT_ready, i * U + h + 1)
                    for w in range(EW):
                        ins = pe.transpose(etile(h, 1, w), pool[h][:, w * C:(w + 1) * C], ident[:, :])
                    ins.then_inc(y_ready, 1)

                def z_rows(i, h):
                    pe.wait_ge(yT_ready, i * U + h + 1)
                    for w in range(EW):
                        pe.matmul(etile(h, 0, w), pool[h][:, w * C:(w + 1) * C], wsi[:, :], start=True, stop=False)
                        ins = pe.matmul(etile(h, 0, w), ones3[:, :], biassi[:, :], start=False, stop=True)
                    ins.then_inc(zz_ready, 1)

                pipeline(pe, U, AT, groups, {"TURN": turn_rows, "FEAT": features, "EP": e_and_pool, "GF": gate_features,
                                                "GATE": gate, "HSUM": h2_rows, "TH": turn_h, "Y": y_rows, "ZZ": z_rows})

            @block.vector
            def _(v):
                def product(i, h):
                    at = i * U + h + 1
                    v.wait_ge(fc_ready, at)
                    wait(v, att_ready, at - U)
                    v.tensor_tensor(e[h][:, :], fs[h][:, :], fd[h][:, :], ALU.mult).then_inc(prod_ready, 1)

                def maxima(i, h):
                    at, g = i * U + h + 1, i * U + h
                    ch = Chain(v, max_link, 2, at)
                    v.wait_ge(e_ready, at)
                    v.wait_ge(loaded[h], 32 * (i + 1))
                    softmax_scans(v, ch, h, g, m, z, r, e, ab, neg, m_done)
                    v.tensor_tensor(ab[h][:, 0, :], ab[h][:, 0, :], m[h][:, 1:EG + 1], ALU.subtract
                                    ).then_inc(ab_ready, 1)
                    wait(v, pm_done, g)
                    wait(v, gf_ready, at - U)
                    first = NEG if isinstance(g, int) and g == 0 else pm[(h - 1) % U][:, EG - 1:EG]
                    v.tensor_tensor_scan(pm[h][:, :], neg[h][:, :], pool[h][:, :], first, ALU.add, ALU.max
                                         ).then_inc(pm_done, 1)

                def weighted(i, h):
                    at, g = i * U + h + 1, i * U + h
                    ch = Chain(v, sum_link, 2, at)
                    v.wait_ge(exp_ready, at)
                    wait(v, z_done, g)
                    v.tensor_tensor_scan(z[h][:, :], ab[h][:, 0, :], ab[h][:, 1, :], last_of(z, h, g), ALU.mult,
                                         ALU.add).then_inc(z_done, 1)
                    ch.link(v.tensor_tensor(fs[h][:, :], fs[h][:, :], ab[h][:, 1, :], ALU.mult))
                    wait(v, r_done, g)
                    v.tensor_tensor_scan(r[h][:, :], ab[h][:, 0, :], fs[h][:, :], last_of(r, h, g), ALU.mult,
                                         ALU.add).then_inc(r_done, 1)
                    v.wait_ge(z_done, at)
                    ch.link(v.reciprocal(e[h][:, :], z[h][:, :]))
                    v.wait_ge(r_done, at)
                    v.tensor_tensor(fd[h][:, :], r[h][:, :], e[h][:, :], ALU.mult).then_inc(agg_ready, 1)

                def attention(i, h):
                    at = i * U + h + 1
                    ch = Chain(v, att_link, 2, at)
                    v.wait_ge(ex_ready, at)
                    ch.link(v.tensor_scalar(ab[h][:, 1, :], ab[h][:, 1, :], 1.0, -1.0, ALU.min, ALU.add))
                    ch.link(v.tensor_tensor(fd[h][:, :], fd[h][:, :], ab[h][:, 1, :], ALU.max))
                    v.scalar_tensor_tensor(out=fd[h][:, :], in0=ab[h][:, 0, :], scalar=1.0, in1=fd[h][:, :],
                                           op0=ALU.add, op1=ALU.mult).then_inc(att_ready, 1)

                def stats_h(i, h):
                    ch = Chain(v, statsh_link, 5, i * U + h + 1)
                    v.wait_ge(h2_ready, i * U + h + 1)
                    wait(v, n3_ready, (i - 1) * U + h + 1)
                    row_stats(v, ch, st[h], small[h], h2[h], EW, True, varh_ready)
                    ch.end()

                def form_x3(i, h):
                    at = i * U + h + 1
                    v.wait_ge(y_ready, at)
                    v.wait_ge(loaded[h], 32 * (i + 1))
                    wait(v, stored[h], 32 * i)
                    v.scalar_tensor_tensor(out=flat(x3[h]), in0=ebank(h, 1), scalar=-1.0, in1=flat(xe[h]), op0=ALU.add,
                                           op1=ALU.add).then_inc(y_used, 1)

                def elu(i, h):
                    at = i * U + h + 1
                    v.wait_ge(ez_ready, at)
                    v.scalar_tensor_tensor(out=e[h][:, :], in0=flat(h2[h]), scalar=1.0, in1=ebank(h, 0), op0=ALU.min,
                                           op1=ALU.max).then_inc(w_done, 1)
                    v.wait_ge(w_done, at)
                    v.wait_ge(y_used, at)
                    v.tensor_tensor(flat(x3[h]), flat(x3[h]), e[h][:, :], ALU.add).then_inc(x3_ready, 1)

                def stats3(i, h):
                    ch = Chain(v, stats3_link, 5, i * U + h + 1)
                    v.wait_ge(x3_ready, i * U + h + 1)
                    v.wait_ge(nh_ready, i * U + h + 1)
                    row_stats(v, ch, st[h], small[h], x3[h], EW, True, var3_ready)
                    ch.end()

                pipeline(v, U, AT, groups, {"PROD": product, "MAXI": maxima, "SUMS": weighted, "ATT": attention,
                                               "STATSH": stats_h, "X3": form_x3, "ELU": elu, "STATS3": stats3})

        with Phase(nc) as phase, ExitStack() as ctx:
            def sem(name):
                return phase.semaphore("l3_" + name)

            def bufs(name, shape, dt=F32):
                return [sb(f"l3_{name}{h}", shape, dt, ctx) for h in range(U)]

            def sems(name):
                return [sem(f"{name}{h}") for h in range(U)]

            xin = bufs("xin", [P, EW, C])
            own = bufs("own", [P, EW, C])
            hT = bufs("hT", [P, 2, EG])
            agg = bufs("agg", [P, EG])
            total = bufs("total", [P, EG])
            same = bufs("same", [P, EG])
            xe = bufs("xe", [P, EW, C])
            scaled = bufs("scaled", [P, EW, C])
            res = bufs("res", [P, EW, C])
            factor = bufs("factor", [P, EW])
            index = bufs("index", [P, 2, EW], I32)
            gathered, scattered, loaded = (sems(n) for n in ("gathered", "scattered", "loaded"))
            (staged, passed, t_ready, hT_ready, agg_done, total_ready, mm_ready, scaled_ready, out_ready,
             scat_staged) = [sem(n) for n in (
                 "staged", "passed", "t_ready", "hT_ready", "agg_done", "total_ready", "mm_ready", "scaled_ready",
                 "out_ready", "scat_staged")]
            factor_ready = sem("factor_ready")
            block = ctx.enter_context(nc.Block())
            AT = dict(INDEX=0.0, GATHER=0.500, LOAD=0.500, TURN=1.701, RELU=1.911, AGG=2.036, MM=2.207, OUT=2.332,
                      PUT=2.995)

            @block.sync
            def _(sp):
                def load(i, h):
                    g = i * U + h
                    wait(sp, out_ready, g + 1 - U)
                    sp.dma_start(own[h][:, :, :], group_rows(n3_e, g)).then_inc(loaded[h], 16)
                    sp.dma_start(xe[h][:, :, :], group_rows(x3_e, g)).then_inc(loaded[h], 16)
                    sp.dma_start(same[h][:, :], mask_row(0, g)).then_inc(loaded[h], 16)

                pipeline(sp, U, AT, groups, {"LOAD": load})

            @block.gpsimd
            def _(g):
                limit = g.to_reg(N - 1)

                def fetch(i, h):
                    at = i * U + h + 1
                    wait(g, t_ready, at - U)
                    g.wait_ge(staged, at)
                    g.sem_inc(passed, 1)
                    gather(g, xin[h], t_n3, index[h][:, 0, :], gathered[h], limit)

                def put(i, h):
                    at = i * U + h + 1
                    g.wait_ge(out_ready, at)
                    g.wait_ge(scat_staged, at)
                    g.sem_inc(passed, 1)
                    scatter(g, out, res[h], index[h][:, 1, :], scattered[h], limit)

                pipeline(g, U, AT, groups, {"GATHER": fetch, "PUT": put})
                for h in range(U):
                    g.wait_ge(scattered[h], 16 * EW * turns(h))

            @block.scalar
            def _(act):
                def relu_t(i, h):
                    at = i * U + h + 1
                    act.wait_ge(t_ready, at)
                    wait(act, total_ready, at - U)
                    act.activation(hT[h][:, :, :], ps[h // 2][:, 1024 * (h % 2):1024 * (h % 2) + 1024].rearrange(
                        "p (k c) -> p k c", k=2), ACT.Relu).then_inc(hT_ready, 1)

                pipeline(act, U, AT, groups, {"RELU": relu_t})

            @block.tensor
            def _(pe):
                def turn_rows(i, h):
                    at = i * U + h + 1
                    pe.wait_ge(gathered[h], 16 * EW * (i + 1))
                    pe.wait_ge(loaded[h], 48 * (i + 1))
                    wait(pe, out_ready, at - U)
                    for w in range(EW):
                        pe.transpose(etile(h, 0, w), xin[h][:, w, :], ident[:, :])
                        ins = pe.transpose(etile(h, 1, w), own[h][:, w, :], ident[:, :])
                    ins.then_inc(t_ready, 1)

                def product(i, h):
                    pe.wait_ge(total_ready, i * U + h + 1)
                    for w in range(EW):
                        ins = pe.matmul(etile(h, 0, w), total[h][:, w * C:(w + 1) * C], w3[:, :], start=True,
                                        stop=True)
                    ins.then_inc(mm_ready, 1)

                pipeline(pe, U, AT, groups, {"TURN": turn_rows, "MM": product})

            @block.vector
            def _(v):
                def indices(i, h):
                    wait(v, gathered[h], 16 * EW * i)
                    stage(v, src_i, index[h][:, 0, :], i * U + h + 1, staged)

                def aggregate(i, h):
                    at, g = i * U + h + 1, i * U + h
                    v.wait_ge(hT_ready, at)
                    v.wait_ge(loaded[h], 48 * (i + 1))
                    wait(v, agg_done, g)
                    v.tensor_tensor_scan(agg[h][:, :], same[h][:, :], hT[h][:, 0, :], last_of(agg, h, g), ALU.mult,
                                         ALU.add).then_inc(agg_done, 1)
                    v.wait_ge(agg_done, at)
                    wait(v, mm_ready, at - U)
                    v.tensor_tensor(total[h][:, :], agg[h][:, :], hT[h][:, 1, :], ALU.add).then_inc(total_ready, 1)

                def form_out(i, h):
                    at = i * U + h + 1
                    v.wait_ge(mm_ready, at)
                    v.tensor_copy(factor[h][:, :], dinv[:, bass.ds((at - 1) * EW, EW)]).then_inc(factor_ready, 1)
                    v.wait_ge(factor_ready, at)
                    for w in range(EW):
                        ins = v.scalar_tensor_tensor(out=scaled[h][:, w, :], in0=etile(h, 0, w),
                                                     scalar=factor[h][:, w:w + 1], in1=b3rows[:, :], op0=ALU.mult,
                                                     op1=ALU.add)
                    ins.then_inc(scaled_ready, 1)
                    v.wait_ge(scaled_ready, at)
                    wait(v, scattered[h], 16 * EW * i)
                    stage(v, scat_i, index[h][:, 1, :], at, scat_staged)
                    v.scalar_tensor_tensor(out=flat(res[h]), in0=flat(scaled[h]), scalar=0.0, in1=flat(xe[h]),
                                           op0=ALU.max, op1=ALU.add).then_inc(out_ready, 1)

                pipeline(v, U, AT, groups, {"INDEX": indices, "AGG": aggregate, "OUT": form_out})


_INS = ['x', 'src', 'dst', 'edge_attr_16', 'L0_gnn_Wq', 'L0_gnn_Wk', 'L0_gnn_Wv', 'L0_gnn_Wres', 'L1_gnn_W',
        'L1_gnn_edge_w', 'L1_gnn_b', 'L2_gnn_ln1_g', 'L2_gnn_ln1_b', 'L2_gnn_W_attn', 'L2_gnn_W_pool',
        'L2_gnn_b_pool', 'L2_gnn_W_gself', 'L2_gnn_W_gneigh', 'L2_gnn_b_gate', 'L2_gnn_W_gr', 'L2_gnn_b_gr',
        'L2_gnn_W_hr', 'L2_gnn_b_hr', 'L2_gnn_ln2_g', 'L2_gnn_ln2_b', 'L2_gnn_W_si', 'L2_gnn_b_si', 'L3_gnn_W',
        'L3_gnn_b']


def kernel(**inputs):
    import numpy as _np
    import concourse.bacc as _bacc
    from concourse import mybir as _mybir
    from concourse.bass_utils import run_bass_kernel_spmd as _run

    nc = _bacc.Bacc("TRN2", target_bir_lowering=False, num_devices=1)
    arrays, args = {}, {}
    for name in _INS:
        v = _np.ascontiguousarray(inputs[name])
        arrays[f"in_{name}_dram"] = v
        args[name] = nc.dram_tensor(f"in_{name}_dram", v.shape, _mybir.dt.from_np(v.dtype), kind="ExternalInput").ap()
    out = nc.dram_tensor("out_0_dram", inputs["x"].shape, _mybir.dt.float32, kind="ExternalOutput").ap()
    bass_gnn(nc, args, out)
    r = _run(nc, [arrays], core_ids=[0])
    return r.results[0]["out_0_dram"]
```
